# Optimizing a Trainium2 kernel written in Bass

```python
import numpy as np
import jax
import jax.numpy as jnp

def _softmax(x, axis=-1):
    return jax.nn.softmax(x, axis=axis)

def _gelu(x):
    return jax.nn.gelu(x, approximate=True)

def _silu(x):
    return jax.nn.silu(x)

def _sigmoid(x):
    return jax.nn.sigmoid(x)

def _layernorm(x, axis=-1, eps=1e-05):
    m = jnp.mean(x, axis=axis, keepdims=True)
    v = jnp.var(x, axis=axis, keepdims=True)
    return (x - m) / jnp.sqrt(v + eps)

def _scatter_add(tgt, idx, src, axis=0):
    return tgt.at[idx].add(src)

def _segment_sum(src, seg, n):
    return jax.ops.segment_sum(src, seg, n)
kernel_name = 'mk_flamingo_gated_d4_seqx_r8_58063b'

def setup_inputs(seed: int=0):
    np.random.seed(seed)
    _w = jnp.asarray

    def _rec_inputs():
        import jax
        import jax.numpy as jnp
        _rk = jax.random.key(seed)
        x = 7.22e-05 + 1 * jax.random.normal(jax.random.fold_in(_rk, 1), (128, 64, 128), jnp.float32)
        _lenS = 64 - jax.random.randint(jax.random.fold_in(_rk, 7), (128,), 0, max(1, 64 // 4) + 1, jnp.int32)
        _lenS2 = 64 - jax.random.randint(jax.random.fold_in(_rk, 8), (128,), 0, max(1, 64 // 4) + 1, jnp.int32)
        _ctx_1024P = jax.random.normal(jax.random.fold_in(_rk, 11), (128, 16, 128), jnp.float32)
        _ctx_1024c = jax.random.dirichlet(jax.random.fold_in(_rk, 511), 0.3 * jnp.ones((16,), jnp.float32), (128, 64))
        _ctx_1024t = jnp.einsum('bsk,bkd->bsd', _ctx_1024c, _ctx_1024P)
        _ctx_1024t = _ctx_1024t * jax.lax.rsqrt(jnp.mean(jnp.square(_ctx_1024t)) + 1e-12) * 0.953939
        ctx_1024 = 4.13588e-05 + 0.999923 * (_ctx_1024t + 0.3 * jax.random.normal(jax.random.fold_in(_rk, 611), (128, 64, 128), jnp.float32))
        _validS = jnp.arange(64)[None, :] < _lenS[:, None]
        _validS2 = jnp.arange(64)[None, :] < _lenS2[:, None]
        _causal = jnp.tril(jnp.ones((64, 64), dtype=bool))
        mask_BxS2_bf1 = jnp.ones((128, 64), dtype=bool)
        _g = jax.random.normal(jax.random.fold_in(_rk, 9001), (2, 4), jnp.float32)
        _g = jnp.sign(_g) * jnp.maximum(jnp.abs(_g), 1.0) + (_g == 0) * 1.0
        g_xattn = _g[0]
        g_ffn = _g[1]
        return (x, ctx_1024, mask_BxS2_bf1, g_xattn, g_ffn)
    x, ctx_1024, mask_BxS2_bf1, g_xattn, g_ffn = _rec_inputs()

    def _L0_xattn_setup():
        import jax, jax.numpy as jnp
        import numpy as np
        D_MODEL = 128
        HEADS = 16
        D_HEAD = D_MODEL // HEADS
        SEQ = 256
        C = 2
        K_TOP = int(C * np.log(SEQ))
        key = jax.random.key(seed)
        ks = jax.random.split(key, 5)
        s = 0.02
        return {'Q': jax.random.normal(ks[0], (4, SEQ, D_MODEL), jnp.float32), 'K': jax.random.normal(ks[1], (4, SEQ, D_MODEL), jnp.float32), 'V': jax.random.normal(ks[2], (4, SEQ, D_MODEL), jnp.float32), 'Wq': jax.random.normal(ks[3], (D_MODEL, D_HEAD), jnp.float32) * s, 'bq': jnp.zeros((D_HEAD,), jnp.float32), 'Wout': jax.random.normal(ks[4], (HEADS * D_HEAD, D_MODEL), jnp.float32) * s, 'bout': jnp.zeros((D_MODEL,), jnp.float32)}
    _L0_xattn_all = _L0_xattn_setup()
    _L0_xattn_in = {k: v for k, v in _L0_xattn_all.items() if k in ('Wq', 'bq', 'Wout', 'bout')}
    del _L0_xattn_all

    def _L0_ffn_setup():
        import jax, jax.numpy as jnp
        import numpy as np
        B, L, D = (4, 256, 128)
        H = 16
        E = 16
        NS = 16
        S = NS // E
        F = 512
        EPS = 1e-05

        def _layernorm(x, g, b):
            mu = jnp.mean(x, axis=-1, keepdims=True)
            var = jnp.mean(jnp.square(x - mu), axis=-1, keepdims=True)
            return (x - mu) * jax.lax.rsqrt(var + EPS) * g + b

        def _mha(q, k, v, Wq, bq, Wk, bk, Wv, bv, Wo, bo):
            Bq, Lq, Dm = q.shape
            dh = Dm // H
            qh = (q @ Wq + bq).reshape(Bq, Lq, H, dh)
            kh = (k @ Wk + bk).reshape(Bq, -1, H, dh)
            vh = (v @ Wv + bv).reshape(Bq, -1, H, dh)
            scores = jnp.einsum('bqhd,bkhd->bhqk', qh, kh) / jnp.asarray(np.sqrt(dh), q.dtype)
            attn = jax.nn.softmax(scores, axis=-1)
            out = jnp.einsum('bhqk,bkhd->bqhd', attn, vh).reshape(Bq, Lq, Dm)
            return out @ Wo + bo
        key = jax.random.key(seed)
        ks = jax.random.split(key, 32)
        s = 0.02
        d = {}
        d['x'] = jax.random.normal(ks[0], (B, L, D), jnp.float32)
        d['slot_query'] = jax.random.normal(ks[1], (1, NS, D), jnp.float32) * 0.01
        for i, nm in enumerate(['d_Wq', 'd_Wk', 'd_Wv', 'd_Wo']):
            d[nm] = jax.random.normal(ks[2 + i], (D, D), jnp.float32) * s
        for nm in ['d_bq', 'd_bk', 'd_bv', 'd_bo']:
            d[nm] = jnp.zeros((D,), jnp.float32)
        for i, nm in enumerate(['c_Wq', 'c_Wk', 'c_Wv', 'c_Wo']):
            d[nm] = jax.random.normal(ks[6 + i], (D, D), jnp.float32) * s
        for nm in ['c_bq', 'c_bk', 'c_bv', 'c_bo']:
            d[nm] = jnp.zeros((D,), jnp.float32)
        d['e_ln_g'] = jnp.ones((E, D), jnp.float32)
        d['e_ln_b'] = jnp.zeros((E, D), jnp.float32)
        d['e_W1'] = jax.random.normal(ks[10], (E, D, F), jnp.float32) * s
        d['e_b1'] = jnp.zeros((E, F), jnp.float32)
        d['e_Wg'] = jax.random.normal(ks[11], (E, D, F), jnp.float32) * s
        d['e_bg'] = jnp.zeros((E, F), jnp.float32)
        d['e_W2'] = jax.random.normal(ks[12], (E, F, D), jnp.float32) * s
        d['e_b2'] = jnp.zeros((E, D), jnp.float32)
        return d
    _L0_ffn_all = _L0_ffn_setup()
    _L0_ffn_in = {k: v for k, v in _L0_ffn_all.items() if k in ('slot_query', 'd_Wq', 'd_Wk', 'd_Wv', 'd_Wo', 'd_bq', 'd_bk', 'd_bv', 'd_bo', 'c_Wq', 'c_Wk', 'c_Wv', 'c_Wo', 'c_bq', 'c_bk', 'c_bv', 'c_bo', 'e_ln_g', 'e_ln_b', 'e_W1', 'e_b1', 'e_Wg', 'e_bg', 'e_W2', 'e_b2')}
    del _L0_ffn_all

    def _L1_xattn_setup():
        import jax, jax.numpy as jnp
        import numpy as np
        import math
        B, S, E = (2, 256, 128)
        H = 16
        DK = E // H
        MAX_DIST = 256

        def _split_heads(x):
            b, s, _ = x.shape
            return x.reshape(b, s, H, DK).transpose(0, 2, 1, 3)
        key = jax.random.key(seed)
        ks = jax.random.split(key, 9)
        sc = 1.0 / math.sqrt(E)
        return {'key': jax.random.normal(ks[0], (B, S, E), jnp.float32), 'query': jax.random.normal(ks[1], (B, S, E), jnp.float32), 'value': jax.random.normal(ks[2], (B, S, E), jnp.float32), 'wq': jax.random.normal(ks[3], (E, E), jnp.float32) * sc, 'wk': jax.random.normal(ks[4], (E, E), jnp.float32) * sc, 'wv': jax.random.normal(ks[5], (E, E), jnp.float32) * sc, 'fc_w': jax.random.normal(ks[6], (E, E), jnp.float32) * sc, 'fc_b': jax.random.normal(ks[7], (E,), jnp.float32) * sc, 'rel_table': jax.random.normal(ks[8], (2 * MAX_DIST - 1, H), jnp.float32) * 0.02}
    _L1_xattn_all = _L1_xattn_setup()
    _L1_xattn_in = {k: v for k, v in _L1_xattn_all.items() if k in ('wq', 'wk', 'wv', 'fc_w', 'fc_b', 'rel_table')}
    del _L1_xattn_all

    def _L1_ffn_setup():
        import jax, jax.numpy as jnp
        import numpy as np
        D_MODEL, D_FF, RANK = (128, 512, 32)
        B, S = (4, 512)
        key = jax.random.key(seed)
        ks = jax.random.split(key, 7)
        return {'x': jax.random.normal(ks[0], (B, S, D_MODEL), dtype=jnp.float32), 'U1': jax.random.normal(ks[1], (D_MODEL, RANK), dtype=jnp.float32) * 0.02, 'V1': jax.random.normal(ks[2], (RANK, D_FF), dtype=jnp.float32) * 0.02, 'b1': jnp.zeros((D_FF,), dtype=jnp.float32), 'U2': jax.random.normal(ks[3], (D_FF, RANK), dtype=jnp.float32) * 0.02, 'V2': jax.random.normal(ks[4], (RANK, D_MODEL), dtype=jnp.float32) * 0.02, 'b2': jnp.zeros((D_MODEL,), dtype=jnp.float32)}
    _L1_ffn_all = _L1_ffn_setup()
    _L1_ffn_in = {k: v for k, v in _L1_ffn_all.items() if k in ('U1', 'V1', 'b1', 'U2', 'V2', 'b2')}
    del _L1_ffn_all

    def _L2_xattn_setup():
        import jax, jax.numpy as jnp
        import numpy as np
        B, T, M, E, H = (8, 64, 128, 128, 8)
        MAX_LEN = 128

        def sinusoidal_table(max_len, n_model):
            pos = jnp.concatenate([jnp.arange(-(max_len // 2), 0, dtype=jnp.float32), jnp.arange(0, max_len // 2, dtype=jnp.float32)])
            inv = 10000.0 ** ((jnp.arange(n_model) // 2 * 2).astype(jnp.float32) / n_model)
            w = pos[:, None] / inv[None, :]
            even = jnp.sin(w[:, 0::2])
            odd = jnp.cos(w[:, 1::2])
            out = jnp.zeros((max_len, n_model), jnp.float32)
            out = out.at[:, 0::2].set(even)
            out = out.at[:, 1::2].set(odd)
            return out
        key = jax.random.key(seed)
        ks = jax.random.split(key, 10)
        s = 0.02
        return {'q': jax.random.normal(ks[0], (B, T, M), jnp.float32), 'k': jax.random.normal(ks[1], (B, T, M), jnp.float32), 'v': jax.random.normal(ks[2], (B, T, M), jnp.float32), 'mask': jnp.ones((B, T), dtype=bool), 'wq': jax.random.normal(ks[3], (M, E, H), jnp.float32) * s, 'wk': jax.random.normal(ks[4], (M, E, H), jnp.float32) * s, 'wv': jax.random.normal(ks[5], (M, E, H), jnp.float32) * s, 'bu': jax.random.normal(ks[6], (E, H), jnp.float32) * s, 'bv': jax.random.normal(ks[7], (E, H), jnp.float32) * s, 'wo': jax.random.normal(ks[8], (E, H, M), jnp.float32) * s, 'pos_w': sinusoidal_table(MAX_LEN, E)}
    _L2_xattn_all = _L2_xattn_setup()
    _L2_xattn_in = {k: v for k, v in _L2_xattn_all.items() if k in ('wq', 'wk', 'wv', 'bu', 'bv', 'wo', 'pos_w')}
    del _L2_xattn_all

    def _L2_ffn_setup():
        import jax, jax.numpy as jnp
        import numpy as np
        BLOCK_SIZE = 32
        FP6_E2M3_MAX = 7.5

        def _build_fp6_e2m3_grid():
            vals = set()
            for bits in range(64):
                s = bits >> 5 & 1
                e = bits >> 3 & 3
                m = bits & 7
                v = m / 8.0 if e == 0 else (1.0 + m / 8.0) * 2.0 ** (e - 1)
                vals.add(-v if s else v)
            return np.array(sorted(vals), dtype=np.float32)
        _GRID = jnp.asarray(_build_fp6_e2m3_grid())

        def _nearest_on_grid(x, grid):
            idx = jnp.clip(jnp.searchsorted(grid, x), 0, grid.shape[0] - 1)
            idx_lo = jnp.maximum(idx - 1, 0)
            v_hi = grid[idx]
            v_lo = grid[idx_lo]
            return jnp.where(jnp.abs(x - v_lo) <= jnp.abs(x - v_hi), v_lo, v_hi)

        def _mx_quantize(t, eps=1e-30):
            rows, K = t.shape
            blocks = t.reshape(rows, K // BLOCK_SIZE, BLOCK_SIZE)
            scales = jnp.maximum(jnp.max(jnp.abs(blocks), axis=-1) / FP6_E2M3_MAX, eps)
            q = _nearest_on_grid(blocks / scales[..., None], _GRID)
            return (q, scales)
        key = jax.random.key(seed)
        k1, k2, k3 = jax.random.split(key, 3)
        x = jax.random.normal(k1, (8, 1024, 128), dtype=jnp.float32)
        weight = jax.random.normal(k2, (128, 128), dtype=jnp.float32) * 0.02
        bias = jax.random.normal(k3, (128,), dtype=jnp.float32) * 0.02
        return {'x': x, 'weight': weight, 'bias': bias}
    _L2_ffn_all = _L2_ffn_setup()
    _L2_ffn_in = {k: v for k, v in _L2_ffn_all.items() if k in ('weight', 'bias')}
    del _L2_ffn_all

    def _L3_xattn_setup():
        import jax, jax.numpy as jnp
        import numpy as np
        B, L_ENC, L_DEC, D = (16, 64, 128, 128)
        key = jax.random.key(seed)
        k1, k2, k3, k4, k5, k6 = jax.random.split(key, 6)
        encoder_hc = jax.random.normal(k1, (B, L_ENC, D), dtype=jnp.float32)
        decoder_hq = jax.random.normal(k2, (B, L_DEC, D), dtype=jnp.float32)
        w_sim = jax.random.normal(k3, (3 * D,), dtype=jnp.float32) * 0.02
        b_sim = jax.random.normal(k4, (1,), dtype=jnp.float32) * 0.02
        W_qv = jax.random.normal(k5, (4 * D, D), dtype=jnp.float32) * 0.02
        b_qv = jax.random.normal(k6, (D,), dtype=jnp.float32) * 0.02
        return {'encoder_hc': encoder_hc, 'decoder_hq': decoder_hq, 'w_sim': w_sim, 'b_sim': b_sim, 'W_qv': W_qv, 'b_qv': b_qv}
    _L3_xattn_all = _L3_xattn_setup()
    _L3_xattn_in = {k: v for k, v in _L3_xattn_all.items() if k in ('w_sim', 'b_sim', 'W_qv', 'b_qv')}
    del _L3_xattn_all

    def _L3_ffn_setup():
        import jax, jax.numpy as jnp
        import numpy as np
        D_MODEL = 128
        HIDDEN = 512
        N_ROUTING = 2
        key = jax.random.key(seed)
        ks = jax.random.split(key, 10)
        s = 0.02
        x = jax.random.normal(ks[0], (4, 512, D_MODEL), dtype=jnp.float32)
        gate_w = jax.random.normal(ks[1], (N_ROUTING, D_MODEL), dtype=jnp.float32) * s
        w1 = jax.random.normal(ks[2], (N_ROUTING, D_MODEL, HIDDEN), dtype=jnp.float32) * s
        b1 = jax.random.normal(ks[3], (N_ROUTING, HIDDEN), dtype=jnp.float32) * s
        w2 = jax.random.normal(ks[4], (N_ROUTING, HIDDEN, D_MODEL), dtype=jnp.float32) * s
        b2 = jax.random.normal(ks[5], (N_ROUTING, D_MODEL), dtype=jnp.float32) * s
        sw1 = jax.random.normal(ks[6], (D_MODEL, HIDDEN), dtype=jnp.float32) * s
        sb1 = jax.random.normal(ks[7], (HIDDEN,), dtype=jnp.float32) * s
        sw2 = jax.random.normal(ks[8], (HIDDEN, D_MODEL), dtype=jnp.float32) * s
        sb2 = jax.random.normal(ks[9], (D_MODEL,), dtype=jnp.float32) * s
        return {'x': x, 'gate_w': gate_w, 'w1': w1, 'b1': b1, 'w2': w2, 'b2': b2, 'sw1': sw1, 'sb1': sb1, 'sw2': sw2, 'sb2': sb2}
    _L3_ffn_all = _L3_ffn_setup()
    _L3_ffn_in = {k: v for k, v in _L3_ffn_all.items() if k in ('gate_w', 'w1', 'b1', 'w2', 'b2', 'sw1', 'sb1', 'sw2', 'sb2')}
    del _L3_ffn_all
    return {'x': x, 'ctx_1024': ctx_1024, 'mask_BxS2_bf1': mask_BxS2_bf1, 'g_xattn': g_xattn, 'g_ffn': g_ffn, 'L0_xattn_Wq': _L0_xattn_in['Wq'], 'L0_xattn_bq': _L0_xattn_in['bq'], 'L0_xattn_Wout': _L0_xattn_in['Wout'], 'L0_xattn_bout': _L0_xattn_in['bout'], 'L0_ffn_slot_query': _L0_ffn_in['slot_query'], 'L0_ffn_d_Wq': _L0_ffn_in['d_Wq'], 'L0_ffn_d_Wk': _L0_ffn_in['d_Wk'], 'L0_ffn_d_Wv': _L0_ffn_in['d_Wv'], 'L0_ffn_d_Wo': _L0_ffn_in['d_Wo'], 'L0_ffn_d_bq': _L0_ffn_in['d_bq'], 'L0_ffn_d_bk': _L0_ffn_in['d_bk'], 'L0_ffn_d_bv': _L0_ffn_in['d_bv'], 'L0_ffn_d_bo': _L0_ffn_in['d_bo'], 'L0_ffn_c_Wq': _L0_ffn_in['c_Wq'], 'L0_ffn_c_Wk': _L0_ffn_in['c_Wk'], 'L0_ffn_c_Wv': _L0_ffn_in['c_Wv'], 'L0_ffn_c_Wo': _L0_ffn_in['c_Wo'], 'L0_ffn_c_bq': _L0_ffn_in['c_bq'], 'L0_ffn_c_bk': _L0_ffn_in['c_bk'], 'L0_ffn_c_bv': _L0_ffn_in['c_bv'], 'L0_ffn_c_bo': _L0_ffn_in['c_bo'], 'L0_ffn_e_ln_g': _L0_ffn_in['e_ln_g'], 'L0_ffn_e_ln_b': _L0_ffn_in['e_ln_b'], 'L0_ffn_e_W1': _L0_ffn_in['e_W1'], 'L0_ffn_e_b1': _L0_ffn_in['e_b1'], 'L0_ffn_e_Wg': _L0_ffn_in['e_Wg'], 'L0_ffn_e_bg': _L0_ffn_in['e_bg'], 'L0_ffn_e_W2': _L0_ffn_in['e_W2'], 'L0_ffn_e_b2': _L0_ffn_in['e_b2'], 'L1_xattn_wq': _L1_xattn_in['wq'], 'L1_xattn_wk': _L1_xattn_in['wk'], 'L1_xattn_wv': _L1_xattn_in['wv'], 'L1_xattn_fc_w': _L1_xattn_in['fc_w'], 'L1_xattn_fc_b': _L1_xattn_in['fc_b'], 'L1_xattn_rel_table': _L1_xattn_in['rel_table'], 'L1_ffn_U1': _L1_ffn_in['U1'], 'L1_ffn_V1': _L1_ffn_in['V1'], 'L1_ffn_b1': _L1_ffn_in['b1'], 'L1_ffn_U2': _L1_ffn_in['U2'], 'L1_ffn_V2': _L1_ffn_in['V2'], 'L1_ffn_b2': _L1_ffn_in['b2'], 'L2_xattn_wq': _L2_xattn_in['wq'], 'L2_xattn_wk': _L2_xattn_in['wk'], 'L2_xattn_wv': _L2_xattn_in['wv'], 'L2_xattn_bu': _L2_xattn_in['bu'], 'L2_xattn_bv': _L2_xattn_in['bv'], 'L2_xattn_wo': _L2_xattn_in['wo'], 'L2_xattn_pos_w': _L2_xattn_in['pos_w'], 'L2_ffn_weight': _L2_ffn_in['weight'], 'L2_ffn_bias': _L2_ffn_in['bias'], 'L3_xattn_w_sim': _L3_xattn_in['w_sim'], 'L3_xattn_b_sim': _L3_xattn_in['b_sim'], 'L3_xattn_W_qv': _L3_xattn_in['W_qv'], 'L3_xattn_b_qv': _L3_xattn_in['b_qv'], 'L3_ffn_gate_w': _L3_ffn_in['gate_w'], 'L3_ffn_w1': _L3_ffn_in['w1'], 'L3_ffn_b1': _L3_ffn_in['b1'], 'L3_ffn_w2': _L3_ffn_in['w2'], 'L3_ffn_b2': _L3_ffn_in['b2'], 'L3_ffn_sw1': _L3_ffn_in['sw1'], 'L3_ffn_sb1': _L3_ffn_in['sb1'], 'L3_ffn_sw2': _L3_ffn_in['sw2'], 'L3_ffn_sb2': _L3_ffn_in['sb2']}

def reference(x, ctx_1024, mask_BxS2_bf1, g_xattn, g_ffn, L0_xattn_Wq, L0_xattn_bq, L0_xattn_Wout, L0_xattn_bout, L0_ffn_slot_query, L0_ffn_d_Wq, L0_ffn_d_Wk, L0_ffn_d_Wv, L0_ffn_d_Wo, L0_ffn_d_bq, L0_ffn_d_bk, L0_ffn_d_bv, L0_ffn_d_bo, L0_ffn_c_Wq, L0_ffn_c_Wk, L0_ffn_c_Wv, L0_ffn_c_Wo, L0_ffn_c_bq, L0_ffn_c_bk, L0_ffn_c_bv, L0_ffn_c_bo, L0_ffn_e_ln_g, L0_ffn_e_ln_b, L0_ffn_e_W1, L0_ffn_e_b1, L0_ffn_e_Wg, L0_ffn_e_bg, L0_ffn_e_W2, L0_ffn_e_b2, L1_xattn_wq, L1_xattn_wk, L1_xattn_wv, L1_xattn_fc_w, L1_xattn_fc_b, L1_xattn_rel_table, L1_ffn_U1, L1_ffn_V1, L1_ffn_b1, L1_ffn_U2, L1_ffn_V2, L1_ffn_b2, L2_xattn_wq, L2_xattn_wk, L2_xattn_wv, L2_xattn_bu, L2_xattn_bv, L2_xattn_wo, L2_xattn_pos_w, L2_ffn_weight, L2_ffn_bias, L3_xattn_w_sim, L3_xattn_b_sim, L3_xattn_W_qv, L3_xattn_b_qv, L3_ffn_gate_w, L3_ffn_w1, L3_ffn_b1, L3_ffn_w2, L3_ffn_b2, L3_ffn_sw1, L3_ffn_sb1, L3_ffn_sw2, L3_ffn_sb2):
    import jax
    import jax.numpy as jnp

    def _L0_xattn_ref(Q, K, V, Wq, bq, Wout, bout):
        import jax, jax.numpy as jnp
        import numpy as np
        D_MODEL = 128
        HEADS = 16
        D_HEAD = D_MODEL // HEADS
        SEQ = 256
        C = 2
        K_TOP = int(C * np.log(SEQ))
        B, L, _ = Q.shape
        q = (Q @ Wq + bq).transpose(0, 2, 1)
        k_ = (K @ Wq + bq).transpose(0, 2, 1)
        v = (V @ Wq + bq).transpose(0, 2, 1)
        Qf = jnp.fft.fft(q.astype(jnp.complex64))
        Kf = jnp.fft.fft(k_.astype(jnp.complex64))
        corr = jnp.real(jnp.fft.ifft(Qf * jnp.conj(Kf)))
        corr = corr.mean(axis=(0, 1))
        W_topk, I_topk = jax.lax.top_k(corr, K_TOP)
        W_topk = jax.nn.softmax(W_topk)

        def body(R, ws):
            w, shift = ws
            return (R + w * jnp.roll(v, -shift, axis=-1), None)
        R3, _ = jax.lax.scan(body, jnp.zeros_like(v), (W_topk, I_topk))
        R = jnp.broadcast_to(R3[:, None], (B, HEADS, D_HEAD, L)).reshape(B, L, HEADS * D_HEAD)
        return R @ Wout + bout

    def _L0_ffn_ref(x, slot_query, d_Wq, d_Wk, d_Wv, d_Wo, d_bq, d_bk, d_bv, d_bo, c_Wq, c_Wk, c_Wv, c_Wo, c_bq, c_bk, c_bv, c_bo, e_ln_g, e_ln_b, e_W1, e_b1, e_Wg, e_bg, e_W2, e_b2):
        import jax, jax.numpy as jnp
        import numpy as np
        B, L, D = (4, 256, 128)
        H = 16
        E = 16
        NS = 16
        S = NS // E
        F = 512
        EPS = 1e-05

        def _layernorm(x, g, b):
            mu = jnp.mean(x, axis=-1, keepdims=True)
            var = jnp.mean(jnp.square(x - mu), axis=-1, keepdims=True)
            return (x - mu) * jax.lax.rsqrt(var + EPS) * g + b

        def _mha(q, k, v, Wq, bq, Wk, bk, Wv, bv, Wo, bo):
            Bq, Lq, Dm = q.shape
            dh = Dm // H
            qh = (q @ Wq + bq).reshape(Bq, Lq, H, dh)
            kh = (k @ Wk + bk).reshape(Bq, -1, H, dh)
            vh = (v @ Wv + bv).reshape(Bq, -1, H, dh)
            scores = jnp.einsum('bqhd,bkhd->bhqk', qh, kh) / jnp.asarray(np.sqrt(dh), q.dtype)
            attn = jax.nn.softmax(scores, axis=-1)
            out = jnp.einsum('bhqk,bkhd->bqhd', attn, vh).reshape(Bq, Lq, Dm)
            return out @ Wo + bo
        Bx = x.shape[0]
        q = jnp.broadcast_to(slot_query, (Bx, NS, D))
        o = q + _mha(q, x, x, d_Wq, d_bq, d_Wk, d_bk, d_Wv, d_bv, d_Wo, d_bo)
        os = o.reshape(Bx, E, S, D)
        h = _layernorm(os, e_ln_g[None, :, None, :], e_ln_b[None, :, None, :])
        u = jax.nn.silu(jnp.einsum('besd,edf->besf', h, e_W1) + e_b1[None, :, None, :])
        g = jax.nn.silu(jnp.einsum('besd,edf->besf', h, e_Wg) + e_bg[None, :, None, :])
        y = jnp.einsum('besf,efd->besd', u * g, e_W2) + e_b2[None, :, None, :]
        o = o + y.reshape(Bx, NS, D)
        out = _mha(x, o, o, c_Wq, c_bq, c_Wk, c_bk, c_Wv, c_bv, c_Wo, c_bo)
        return out

    def _L1_xattn_ref(key, query, value, wq, wk, wv, fc_w, fc_b, rel_table):
        import jax, jax.numpy as jnp
        import numpy as np
        import math
        B, S, E = (2, 256, 128)
        H = 16
        DK = E // H
        MAX_DIST = 256

        def _split_heads(x):
            b, s, _ = x.shape
            return x.reshape(b, s, H, DK).transpose(0, 2, 1, 3)
        b, s, _ = query.shape
        k = _split_heads(key @ wk.T)
        q = _split_heads(query @ wq.T)
        v = _split_heads(value @ wv.T)
        ctx = jnp.arange(s)[:, None]
        mem = jnp.arange(s)[None, :]
        rel = jnp.clip(mem - ctx, -MAX_DIST + 1, MAX_DIST - 1) + MAX_DIST - 1
        bias = rel_table[rel]
        bias = bias.transpose(2, 0, 1)[None]
        scores = jnp.einsum('bhqd,bhkd->bhqk', q, k) / math.sqrt(DK)
        scores = scores + bias
        attn = jax.nn.softmax(scores, axis=-1)
        out = jnp.einsum('bhqk,bhkd->bhqd', attn, v)
        out = out.transpose(0, 2, 1, 3).reshape(b, s, E)
        return out @ fc_w.T + fc_b

    def _L1_ffn_ref(x, U1, V1, b1, U2, V2, b2):
        import jax, jax.numpy as jnp
        import numpy as np
        D_MODEL, D_FF, RANK = (128, 512, 32)
        B, S = (4, 512)
        P = jnp.einsum('bsd,dr->bsr', x, U1)
        H = jax.nn.gelu(jnp.einsum('bsr,rf->bsf', P, V1) + b1)
        Q = jnp.einsum('bsf,fr->bsr', H, U2)
        return jnp.einsum('bsr,rd->bsd', Q, V2) + b2

    def _L2_xattn_ref(q, k, v, mask, wq, wk, wv, bu, bv, wo, pos_w):
        import jax, jax.numpy as jnp
        import numpy as np
        B, T, M, E, H = (8, 64, 128, 128, 8)
        MAX_LEN = 128

        def sinusoidal_table(max_len, n_model):
            pos = jnp.concatenate([jnp.arange(-(max_len // 2), 0, dtype=jnp.float32), jnp.arange(0, max_len // 2, dtype=jnp.float32)])
            inv = 10000.0 ** ((jnp.arange(n_model) // 2 * 2).astype(jnp.float32) / n_model)
            w = pos[:, None] / inv[None, :]
            even = jnp.sin(w[:, 0::2])
            odd = jnp.cos(w[:, 1::2])
            out = jnp.zeros((max_len, n_model), jnp.float32)
            out = out.at[:, 0::2].set(even)
            out = out.at[:, 1::2].set(odd)
            return out
        scale = jnp.float32(E) ** 0.5
        qh = jnp.einsum('btm,meh->bteh', q, wq)
        kh = jnp.einsum('btm,meh->bteh', k, wk)
        vh = jnp.einsum('btm,meh->bteh', v, wv)
        t = q.shape[1]
        offset = MAX_LEN // 2 + MAX_LEN % 2
        pos = jnp.arange(t)
        idx = pos[None, :] - pos[:, None] + offset
        p = pos_w[idx]
        attn = jnp.einsum('bqeh,bkeh->bqkh', qh + bu, kh) + jnp.einsum('bqeh,qke->bqkh', qh + bv, p)
        attn = attn / scale
        attn = jnp.where(mask[:, None, :, None], attn, -jnp.inf)
        attn = jax.nn.softmax(attn, axis=-2)
        x = jnp.einsum('bqkh,bkeh->bqeh', attn, vh)
        return jnp.einsum('bqeh,ehm->bqm', x, wo)

    def _L2_ffn_ref(x, weight, bias):
        import jax, jax.numpy as jnp
        import numpy as np
        BLOCK_SIZE = 32
        FP6_E2M3_MAX = 7.5

        def _build_fp6_e2m3_grid():
            vals = set()
            for bits in range(64):
                s = bits >> 5 & 1
                e = bits >> 3 & 3
                m = bits & 7
                v = m / 8.0 if e == 0 else (1.0 + m / 8.0) * 2.0 ** (e - 1)
                vals.add(-v if s else v)
            return np.array(sorted(vals), dtype=np.float32)
        _GRID = jnp.asarray(_build_fp6_e2m3_grid())

        def _nearest_on_grid(x, grid):
            idx = jnp.clip(jnp.searchsorted(grid, x), 0, grid.shape[0] - 1)
            idx_lo = jnp.maximum(idx - 1, 0)
            v_hi = grid[idx]
            v_lo = grid[idx_lo]
            return jnp.where(jnp.abs(x - v_lo) <= jnp.abs(x - v_hi), v_lo, v_hi)

        def _mx_quantize(t, eps=1e-30):
            rows, K = t.shape
            blocks = t.reshape(rows, K // BLOCK_SIZE, BLOCK_SIZE)
            scales = jnp.maximum(jnp.max(jnp.abs(blocks), axis=-1) / FP6_E2M3_MAX, eps)
            q = _nearest_on_grid(blocks / scales[..., None], _GRID)
            return (q, scales)
        batch_shape = x.shape[:-1]
        in_features = x.shape[-1]
        x2 = x.astype(jnp.float32).reshape(-1, in_features)
        w2 = weight.astype(jnp.float32)
        xq, xs = _mx_quantize(x2)
        wq, ws = _mx_quantize(w2)
        xd = (xq * xs[..., None]).reshape(x2.shape)
        wd = (wq * ws[..., None]).reshape(w2.shape)
        out = xd @ wd.T + bias
        return out.reshape(*batch_shape, -1)

    def _L3_xattn_ref(encoder_hc, decoder_hq, w_sim, b_sim, W_qv, b_qv):
        import jax, jax.numpy as jnp
        import numpy as np
        B, L_ENC, L_DEC, D = (16, 64, 128, 128)
        d = encoder_hc.shape[-1]
        w1, w2, w3 = (w_sim[:d], w_sim[d:2 * d], w_sim[2 * d:])
        Sim = (encoder_hc @ w1)[:, :, None] + (decoder_hq @ w2)[:, None, :] + jnp.einsum('bid,bjd->bij', encoder_hc * w3, decoder_hq) + b_sim[0]
        A = jax.nn.softmax(Sim, axis=2)
        hq_hat = jnp.einsum('bij,bjd->bid', A, decoder_hq)
        Batt = jax.nn.softmax(jnp.max(Sim, axis=2), axis=1)
        hc_bar = jnp.einsum('bi,bid->bd', Batt, encoder_hc)[:, None, :]
        hc_hat = jnp.broadcast_to(hc_bar, encoder_hc.shape)
        feats = jnp.concatenate([encoder_hc, hq_hat, encoder_hc * hq_hat, encoder_hc * hc_hat], axis=-1)
        hcq = feats @ W_qv + b_qv
        return hcq

    def _L3_ffn_ref(x, gate_w, w1, b1, w2, b2, sw1, sb1, sw2, sb2):
        import jax, jax.numpy as jnp
        import numpy as np
        D_MODEL = 128
        HIDDEN = 512
        N_ROUTING = 2
        B, S, D = x.shape
        xf = x.reshape(-1, D)
        gate_scores = xf @ gate_w.T
        gate_probs = jax.nn.softmax(gate_scores, axis=-1)
        top1 = jnp.argmax(gate_probs, axis=-1)
        one_hot = jax.nn.one_hot(top1, N_ROUTING, dtype=xf.dtype)
        masked = xf[None, :, :] * one_hot.T[:, :, None]
        h = jax.nn.relu(jnp.einsum('end,edh->enh', masked, w1) + b1[:, None, :])
        expert_out = jnp.einsum('enh,ehd->end', h, w2) + b2[:, None, :]
        routing_output = expert_out.sum(axis=0)
        shared = jax.nn.relu(xf @ sw1 + sb1) @ sw2 + sb2
        return (routing_output + shared).reshape(B, S, D)
    x = x + jnp.tanh(g_xattn[0]) * _L0_xattn_ref(_layernorm(x, axis=-1), ctx_1024, ctx_1024, L0_xattn_Wq, L0_xattn_bq, L0_xattn_Wout, L0_xattn_bout)
    x = x + jnp.tanh(g_ffn[0]) * _L0_ffn_ref(_layernorm(x, axis=-1), L0_ffn_slot_query, L0_ffn_d_Wq, L0_ffn_d_Wk, L0_ffn_d_Wv, L0_ffn_d_Wo, L0_ffn_d_bq, L0_ffn_d_bk, L0_ffn_d_bv, L0_ffn_d_bo, L0_ffn_c_Wq, L0_ffn_c_Wk, L0_ffn_c_Wv, L0_ffn_c_Wo, L0_ffn_c_bq, L0_ffn_c_bk, L0_ffn_c_bv, L0_ffn_c_bo, L0_ffn_e_ln_g, L0_ffn_e_ln_b, L0_ffn_e_W1, L0_ffn_e_b1, L0_ffn_e_Wg, L0_ffn_e_bg, L0_ffn_e_W2, L0_ffn_e_b2)
    x = x + jnp.tanh(g_xattn[1]) * _L1_xattn_ref(ctx_1024, _layernorm(x, axis=-1), ctx_1024, L1_xattn_wq, L1_xattn_wk, L1_xattn_wv, L1_xattn_fc_w, L1_xattn_fc_b, L1_xattn_rel_table)
    x = x + jnp.tanh(g_ffn[1]) * _L1_ffn_ref(_layernorm(x, axis=-1), L1_ffn_U1, L1_ffn_V1, L1_ffn_b1, L1_ffn_U2, L1_ffn_V2, L1_ffn_b2)
    x = x + jnp.tanh(g_xattn[2]) * _L2_xattn_ref(_layernorm(x, axis=-1), ctx_1024, ctx_1024, mask_BxS2_bf1, L2_xattn_wq, L2_xattn_wk, L2_xattn_wv, L2_xattn_bu, L2_xattn_bv, L2_xattn_wo, L2_xattn_pos_w)
    x = x + jnp.tanh(g_ffn[2]) * _L2_ffn_ref(_layernorm(x, axis=-1), L2_ffn_weight, L2_ffn_bias)
    x = x + jnp.tanh(g_xattn[3]) * _L3_xattn_ref(_layernorm(x, axis=-1), ctx_1024, L3_xattn_w_sim, L3_xattn_b_sim, L3_xattn_W_qv, L3_xattn_b_qv)
    x = x + jnp.tanh(g_ffn[3]) * _L3_ffn_ref(_layernorm(x, axis=-1), L3_ffn_gate_w, L3_ffn_w1, L3_ffn_b1, L3_ffn_w2, L3_ffn_b2, L3_ffn_sw1, L3_ffn_sb1, L3_ffn_sw2, L3_ffn_sb2)
    return x

_drawn_inputs = setup_inputs


def setup_inputs(seed=0):
    import zlib

    import numpy as np

    out = dict(_drawn_inputs(seed))
    spreads = {'L0_xattn_bq': (0.0, 0.343),
     'L0_xattn_bout': (0.0, 0.1),
     'L0_ffn_d_bq': (0.0, 0.8),
     'L0_ffn_d_bk': (0.0, 2.0),
     'L0_ffn_d_bv': (0.0, 0.8),
     'L0_ffn_d_bo': (0.0, 0.8),
     'L0_ffn_c_bq': (0.0, 0.8),
     'L0_ffn_c_bk': (0.0, 2.0),
     'L0_ffn_c_bv': (0.0, 2.0),
     'L0_ffn_c_bo': (0.0, 0.8),
     'L0_ffn_e_ln_g': (1.0, 0.6),
     'L0_ffn_e_ln_b': (0.0, 0.8),
     'L0_ffn_e_b1': (0.0, 0.8),
     'L0_ffn_e_bg': (0.0, 0.8),
     'L0_ffn_e_b2': (0.0, 0.8),
     'L1_ffn_b1': (0.0, 0.8),
     'L1_ffn_b2': (0.0, 0.8)}
    factors = {'g_ffn': 8.0,
     'L0_xattn_Wq': 2.916,
     'L0_ffn_slot_query': 8.0,
     'L0_ffn_d_Wq': 8.0,
     'L0_ffn_d_Wk': 8.0,
     'L0_ffn_d_Wv': 8.0,
     'L0_ffn_d_Wo': 8.0,
     'L0_ffn_c_Wq': 8.0,
     'L0_ffn_c_Wk': 8.0,
     'L0_ffn_c_Wv': 8.0,
     'L0_ffn_c_Wo': 4.162,
     'L0_ffn_e_W1': 8.0,
     'L0_ffn_e_Wg': 8.0,
     'L0_ffn_e_W2': 8.0,
     'L1_xattn_rel_table': 64.0,
     'L1_ffn_U1': 8.0,
     'L1_ffn_V1': 8.0,
     'L1_ffn_U2': 8.0,
     'L1_ffn_V2': 8.0,
     'L2_xattn_wq': 64.0,
     'L2_xattn_wk': 64.0,
     'L2_xattn_bu': 64.0,
     'L2_xattn_bv': 64.0,
     'L2_xattn_pos_w': 64.0,
     'L2_ffn_bias': 92.446,
     'L3_xattn_w_sim': 28.672,
     'L3_xattn_b_qv': 97.035,
     'L3_ffn_b1': 64.0,
     'L3_ffn_sb1': 64.0,
     'L3_ffn_sb2': 92.65,
     'L1_xattn_wq': 8.0,
     'L1_xattn_wk': 8.0,
     'L1_xattn_wv': 3.348,
     'L1_xattn_fc_w': 3.379,
     'L1_xattn_fc_b': 8.0,
     'L2_xattn_wv': 8.0,
     'L2_xattn_wo': 8.0,
     'L2_ffn_weight': 8.0,
     'L3_xattn_W_qv': 7.501,
     'L3_ffn_gate_w': 8.0,
     'L3_ffn_w1': 8.0,
     'L3_ffn_w2': 8.0,
     'L3_ffn_b2': 64.0,
     'L3_ffn_sw1': 8.0,
     'L3_ffn_sw2': 8.0}
    for name, (base, spread) in spreads.items():
        noise = np.random.default_rng([zlib.crc32(name.encode()), seed]).standard_normal(out[name].shape)
        drawn = base * np.exp(spread * noise) if base else spread * noise
        out[name] = jnp.asarray(drawn.astype(out[name].dtype))
    for name, factor in factors.items():
        out[name] = (out[name] * factor).astype(out[name].dtype)
    return out
```

```python
import concourse.bass as bass
from concourse import mybir
from contextlib import ExitStack

F32 = mybir.dt.float32
I32 = mybir.dt.int32
U32 = mybir.dt.uint32
ALU = mybir.AluOpType
ACT = mybir.ActivationFunctionType
AX = mybir.AxisListType

P = 128
D = 128
S = 64
B = 128
TILES = B * S // P
T = 4
ROUNDS = TILES // T
RT = T * P
NB = T * 2
EPS = 1e-5
HUGE = 3.0e38


class Counter:

    def __init__(self, sem, base, n, credit):
        self.sem, self.base, self.n, self.credit = sem, base, n, credit

    def now(self, r, k=None):
        return self.sem, r * self.n + (self.base + (self.n if k is None else k))

    def ago(self, r, back, k=None):
        return self.sem, r * self.n + (self.base - back * self.n + (self.n if k is None else k))


class Kit:

    def __init__(self, nc, ctx):
        self.nc, self.ctx, self.sems, self.totals = nc, ctx, {}, {}

    def semaphore(self, name):
        if name not in self.sems:
            self.sems[name] = self.ctx.enter_context(self.nc.semaphore(name))
            self.totals[name] = 0
        return self.sems[name]

    def counter(self, name, n=1, rounds=ROUNDS, back=2):
        sem = self.semaphore(name)
        credit = max(0, back * n - self.totals[name])
        base = self.totals[name] + credit
        self.totals[name] = base + n * rounds
        return Counter(sem, base, n, credit)

    def once(self, name, n=1):
        return self.counter(name, n, 1, 0)


def opens(eng, *counters):
    for s in counters:
        if s.credit:
            eng.sem_inc(s.sem, s.credit)
            s.credit = 0


def every_round(eng, front, main):
    front(0, 0)
    with eng.Fori(0, ROUNDS // 2 - 1) as j:
        front(j * 2 + 1, 1)
        main(j * 2, 0)
        front(j * 2 + 2, 0)
        main(j * 2 + 1, 1)
    front(ROUNDS - 1, 1)
    main(ROUNDS - 2, 0)
    main(ROUNDS - 1, 1)


def every_round_within(eng, front, main):
    front(0, 0)
    front(1, 1)
    with eng.Fori(0, ROUNDS // 2 - 1) as j:
        main(j * 2, 0, lambda: front(j * 2 + 2, 0))
        main(j * 2 + 1, 1, lambda: front(j * 2 + 3, 1))
    main(ROUNDS - 2, 0, lambda: None)
    main(ROUNDS - 1, 1, lambda: None)


def next_round_within(eng, front, main, first=()):
    front(0, 0)
    for step in first:
        front(0, 0, step)
    with eng.Fori(0, ROUNDS // 2 - 1) as j:
        main(j * 2, 0, lambda *step: front(j * 2 + 1, 1, *step))
        main(j * 2 + 1, 1, lambda *step: front(j * 2 + 2, 0, *step))
    main(ROUNDS - 2, 0, lambda *step: front(ROUNDS - 1, 1, *step))
    main(ROUNDS - 1, 1, lambda *step: None)


def staggered(eng, norm, front, main):
    norm(0, 0)
    front(0, 0)
    norm(1, 1)
    with eng.Fori(0, ROUNDS // 2 - 1) as j:
        main(j * 2, 0, lambda *step: front(j * 2 + 1, 1, *step), lambda *step: norm(j * 2 + 2, 0, *step))
        main(j * 2 + 1, 1, lambda *step: front(j * 2 + 2, 0, *step), lambda *step: norm(j * 2 + 3, 1, *step))
    main(ROUNDS - 2, 0, lambda *step: front(ROUNDS - 1, 1, *step), lambda *step: None)
    main(ROUNDS - 1, 1, lambda *step: None, lambda *step: None)


def nothing(r, p):
    pass


def row_on_all(ap, n, offset=0):
    return bass.AP(tensor=ap.tensor, offset=offset, ap=[[0, P], [1, n]])


def column(ap, n=P, offset=0):
    return bass.AP(tensor=ap.tensor, offset=offset, ap=[[1, n], [1, 1]])


def load_table(k, act, func):
    used = k.once("table_in")
    act.activation(k.spare[:, :], k.eps[:, :], func).then_inc(used.sem, 1)
    act.wait_ge(*used.now(0))


class Scope:

    def __init__(self, nc, ctx, tag):
        self.nc, self.ctx, self.tag = nc, ctx, tag

    def sb(self, name, shape, dt=F32):
        return self.ctx.enter_context(self.nc.sbuf_tensor(f"{self.tag}_{name}", shape, dt))

    def banks(self, name, count=1):
        return [self.ctx.enter_context(self.nc.psum_tensor(f"{self.tag}_{name}{i}", [P, 512], F32))
                for i in range(count)]


class Norm:

    def __init__(self, k, m, t_bank, z_read=None):
        sg = k.counter
        self.k, self.bank = k, t_bank
        self.stats, self.moments = sg("stats", T), sg("moments", T)
        self.eps_added, self.rstd = sg("eps_added"), sg("rstd")
        self.normed = sg("normed", T)
        if t_bank is not None:
            self.turned, self.ready = sg("z_turned"), sg("zT_ready")
        self.z_read = z_read or self.turned
        self.st = m.sb("st", [P, T, 6])
        self.mv = [m.sb(f"mv{p}", [P, T, 2]) for p in range(2)]
        self.ve = [m.sb(f"ve{p}", [P, T]) for p in range(2)]
        self.rs = [m.sb(f"rs{p}", [P, T]) for p in range(2)]
        self.z = [m.sb(f"z{p}", [P, T, D]) for p in range(2)]
        self.zT = [m.sb(f"zT{p}", [P, RT]) for p in range(2)]

    def vector(self, v, r, p):
        self.statistics(v, r, p)
        self.finish(v, r, p)

    def statistics(self, v, r, p):
        k = self.k
        for t in range(T):
            v.bn_stats(self.st[:, t, :], k.x[:, r * T + t, :]).then_inc(self.stats.sem, 1)
        v.wait_ge(*self.stats.now(r))
        k.paced(v)
        for t in range(T):
            v.bn_aggr(self.mv[p][:, t, :], self.st[:, t, :]).then_inc(self.moments.sem, 1)

    def finish(self, v, r, p):
        k = self.k
        v.wait_ge(*self.z_read.ago(r, 2))
        v.wait_ge(*self.rstd.now(r))
        for t in range(T):
            v.tensor_scalar(self.z[p][:, t, :], k.x[:, r * T + t, :], self.mv[p][:, t, 0:1],
                            self.rs[p][:, t:t + 1], ALU.subtract, ALU.mult).then_inc(self.normed.sem, 1)

    def pool(self, g, r, p):
        g.wait_ge(*self.moments.now(r))
        g.tensor_tensor(self.ve[p][:, :], self.mv[p][:, :, 1], self.k.eps[:, 0:T], ALU.add)\
            .then_inc(self.eps_added.sem, 1)
        g.wait_ge(*self.eps_added.now(r))
        g.tensor_tensor(self.rs[p][:, :], self.ve[p][:, :], self.k.minus_half[:, 0:T], ALU.pow)\
            .then_inc(self.rstd.sem, 1)

    def tensor(self, pe, r, p):
        pe.wait_ge(*self.ready.ago(r, 1))
        for t in range(T):
            pe.wait_ge(*self.normed.now(r, t + 1))
            last = pe.transpose(self.bank[:, t * P:(t + 1) * P], self.z[p][:, t, :], self.k.ident[:, :])
        last.then_inc(self.turned.sem, 1)

    def scalar(self, a, r, p, *users):
        for u in users:
            a.wait_ge(*u.ago(r, 2))
        a.wait_ge(*self.turned.now(r))
        a.activation(self.zT[p][:, :], self.bank[:, :], ACT.Identity).then_inc(self.ready.sem, 1)

    def opened_by_vector(self):
        return self.stats, self.moments, self.normed


def setup(k, m, io):
    nc = k.nc
    k.x = m.sb("x", [P, TILES, D])
    k.c = m.sb("c", [P, TILES, D])
    k.cT = m.sb("cT", [P, TILES * P])
    k.ident = m.sb("ident", [P, P])
    k.eps = m.sb("eps", [P, 16])
    k.spare = m.sb("spare", [P, 16])
    k.minus_half = m.sb("minus_half", [P, 16])
    k.by8 = m.sb("by8", [P, 16])
    k.by16 = m.sb("by16", [P, 8])
    k.gate_in = m.sb("gate_in", [P, 8])
    k.gate = m.sb("gate", [P, 8])
    pace = {id(e): k.semaphore(f"paced_{n}") for n, e in
            (("dve", nc.vector), ("act", nc.scalar), ("pe", nc.tensor), ("pool", nc.gpsimd))}

    def paced(eng):
        eng.sem_inc(pace[id(eng)], 1)
    k.paced = paced
    cleared, built, loaded, gated = k.once("cleared", 5), k.once("built", 5), k.once("loaded", 16 * 10), k.once("gated")
    with nc.Block() as block:
        @block.sync
        def _(sp):
            for q in range(4):
                rows = slice(q * TILES // 4, (q + 1) * TILES // 4)
                b = slice(q * B // 4, (q + 1) * B // 4)
                for dst, src in ((k.c, io["ctx_1024"]), (k.x, io["x"])):
                    sp.dma_start(dst[:, rows, :], src[b].rearrange("(t b) s d -> (b s) t d", b=2))\
                        .then_inc(loaded.sem, 16)
            sp.dma_start(k.gate_in[:, 0:4], row_on_all(io["g_xattn"], 4)).then_inc(loaded.sem, 16)
            sp.dma_start(k.gate_in[:, 4:8], row_on_all(io["g_ffn"], 4)).then_inc(loaded.sem, 16)

        @block.scalar
        def _(a):
            a.wait_ge(*loaded.now(0))
            a.activation(k.gate[:, :], k.gate_in[:, :], ACT.Tanh).then_inc(gated.sem, 1)

        @block.gpsimd
        def _(g):
            g.memset(k.ident[:, :], 0.0).then_inc(cleared.sem, 1)
            g.memset(k.by8[:, :], 1.0).then_inc(cleared.sem, 1)
            g.memset(k.by16[:, :], 1.0).then_inc(cleared.sem, 1)
            g.memset(k.eps[:, :], EPS).then_inc(cleared.sem, 1)
            g.memset(k.minus_half[:, :], -0.5).then_inc(cleared.sem, 1)
            g.wait_ge(*cleared.now(0))
            g.affine_select(out=k.ident[:, :], in_=k.ident[:, :], compare_op=ALU.not_equal, fill=1.0,
                            base=0, pattern=[[-1, P]], channel_multiplier=1).then_inc(built.sem, 1)
            for n, (mask, w) in enumerate(((k.by8, 8), (k.by16, 16))):
                heads = P // w
                g.affine_select(out=mask[:, :], in_=mask[:, :], compare_op=ALU.is_ge, fill=0.0,
                                base=0, pattern=[[-w, heads]], channel_multiplier=1).then_inc(built.sem, 1)
                g.wait_ge(*built.now(0, 2 * n + 2))
                g.affine_select(out=mask[:, :], in_=mask[:, :], compare_op=ALU.is_ge, fill=0.0,
                                base=w - 1, pattern=[[w, heads]], channel_multiplier=-1).then_inc(built.sem, 1)
            g.wait_ge(*built.now(0))


def turn_context(k, io):
    nc = k.nc
    with ExitStack() as ctx:
        m = Scope(nc, ctx, "tc")
        staged = [m.sb(f"staged{p}", [P, T, D]) for p in range(2)]
        banks = m.banks("bank", 2)
        c_staged, c_turned, cT_ready = k.counter("c_staged"), k.counter("c_turned"), k.counter("cT_ready")
        block = ctx.enter_context(nc.Block())

        @block.gpsimd
        def _(g):
            opens(g, c_staged)

            def stage(r, p):
                g.wait_ge(*c_turned.ago(r, 2))
                k.paced(g)
                g.tensor_copy(staged[p][:, :, :], k.c[:, bass.ds(r * T, T), :]).then_inc(c_staged.sem, 1)
            every_round(g, nothing, stage)

        @block.tensor
        def _(pe):
            opens(pe, c_turned)

            def turn(r, p):
                pe.wait_ge(*cT_ready.ago(r, 2))
                pe.wait_ge(*c_staged.now(r))
                for t in range(T):
                    last = pe.transpose(banks[p][:, t * P:(t + 1) * P], staged[p][:, t, :], k.ident[:, :])
                last.then_inc(c_turned.sem, 1)
            every_round(pe, nothing, turn)

        @block.scalar
        def _(a):
            opens(a, cT_ready)

            def copy(r, p):
                a.wait_ge(*c_turned.now(r))
                k.paced(a)
                a.activation(k.cT[:, bass.ds(r * RT, RT)], banks[p][:, :], ACT.Identity)\
                    .then_inc(cT_ready.sem, 1)
            every_round(a, nothing, copy)


def store(k, io):
    stored = k.once("stored", 16 * 4)
    with k.nc.Block() as block:
        @block.sync
        def _(sp):
            for q in range(4):
                rows = slice(q * TILES // 4, (q + 1) * TILES // 4)
                b = slice(q * B // 4, (q + 1) * B // 4)
                sp.dma_start(io["out"][b].rearrange("(t b) s d -> (b s) t d", b=2), k.x[:, rows, :])\
                    .then_inc(stored.sem, 16)
            sp.wait_ge(*stored.now(0))


def correlation_attention(k, io):
    nc = k.nc
    C8 = 8
    TOP = 11
    with ExitStack() as ctx:
        m = Scope(nc, ctx, "l0x")
        wq = m.sb("wq", [P, C8])
        bq = m.sb("bq", [C8, 1])
        bank_z = m.banks("bank_z")[0]
        bank8 = m.banks("bank8")[0]
        bank_n = m.banks("bank_n", 2)
        norm = Norm(k, m, bank_z)
        small = [m.sb(f"small{i}", [C8, RT]) for i in range(2)]
        nat = {n: m.sb(f"nat_{n}", [P, TILES, C8]) for n in "kq"}
        sg = k.counter
        done8, small_ready = sg("done8", 2), sg("small_ready", 2)
        back, nat_ready = sg("back8", 2), sg("nat_ready", 2)
        loaded = k.once("weights", 32)
        with nc.Block() as block:
            @block.sync
            def _(sp):
                sp.dma_start(wq[:, :], io["L0_xattn_Wq"]).then_inc(loaded.sem, 16)
                sp.dma_start(bq[:, :], column(io["L0_xattn_bq"], C8), allow_slow_non_contiguous=True)\
                    .then_inc(loaded.sem, 16)

            @block.vector
            def _(v):
                opens(v, *norm.opened_by_vector(), nat_ready)

                def main(r, p, next_front):
                    next_front()
                    for n, what in enumerate("kq"):
                        v.wait_ge(*back.now(r, n + 1))
                        v.tensor_scalar(nat[what][:, bass.ds(r * T, T), :],
                                            bank_n[n][:, 0:T * C8].rearrange("p (t c) -> p t c", t=T),
                                            1.0, None, ALU.mult).then_inc(nat_ready.sem, 1)
                every_round_within(v, lambda r, p: norm.vector(v, r, p), main)

            @block.gpsimd
            def _(g):
                opens(g, norm.eps_added, norm.rstd)
                every_round(g, lambda r, p: norm.pool(g, r, p), nothing)

            @block.scalar
            def _(a):
                opens(a, norm.ready, small_ready)
                a.wait_ge(*loaded.now(0))

                def main(r, p):
                    for n in range(2):
                        a.wait_ge(*done8.now(r, n + 1))
                        a.wait_ge(*back.ago(r, 1, n + 1))
                        a.activation(small[n][:, :], bank8[0:C8, :], ACT.Identity, bias=bq[:, 0:1])\
                            .then_inc(small_ready.sem, 1)
                every_round(a, lambda r, p: norm.scalar(a, r, p, done8), main)

            @block.tensor
            def _(pe):
                opens(pe, norm.turned, done8, back)
                pe.wait_ge(*loaded.now(0))

                def main(r, p):
                    for n in range(2):
                        pe.wait_ge(*(small_ready.now(r, n) if n else small_ready.ago(r, 1)))
                        if n:
                            pe.wait_ge(*norm.ready.now(r))
                        k.paced(pe)
                        pe.matmul(bank8[0:C8, :], wq[:, :],
                                  norm.zT[p][:, :] if n else k.cT[:, bass.ds(r * RT, RT)],
                                  start=True, stop=True).then_inc(done8.sem, 1)
                        pe.wait_ge(*nat_ready.ago(r, 1, n + 1))
                        pe.wait_ge(*small_ready.now(r, n + 1))
                        k.paced(pe)
                        for t in range(T):
                            last = pe.transpose(bank_n[n][:, t * C8:(t + 1) * C8],
                                                small[n][:, t * P:(t + 1) * P], k.ident[0:C8, 0:C8])
                        last.then_inc(back.sem, 1)
                every_round(pe, lambda r, p: norm.tensor(pe, r, p), main)

        G16 = TILES // 16
        gt = {n: m.sb(f"gt_{n}", [P, G16, P]) for n in "kq"}
        g_sb = m.sb("g_sb", [P, S])
        diag = m.sb("diag", [S, S])
        mean = m.sb("mean", [S, P])
        corr = m.sb("corr", [P, S])
        rest = m.sb("rest", [P, S])
        best = m.sb("best", [P, 16])
        at = m.sb("at", [P, 16], U32)
        atf = m.sb("atf", [P, 16])
        first = m.sb("first", [P, 1])
        wts, wsum, wrec = m.sb("wts", [P, TOP]), m.sb("wsum", [P, 1]), m.sb("wrec", [P, 1])
        lag_i = m.sb("lag_i", [S, P], I32)
        lag = m.sb("lag", [S, P])
        part = m.sb("part", [S, P])
        circ = m.sb("circ", [S, P])
        wout = m.sb("wout", [S, 2, D])
        mixed = m.sb("mixed", [P, 2, D])
        bout = m.sb("bout", [P, D])
        rows_summed = k.once("rows_summed", 2)
        rows4 = m.sb("rows4", [P, 4, D])
        g_dram = nc.dram_tensor("g_twice", [2 * S + 2, S], F32, kind="Internal")
        r_dram = nc.dram_tensor("rows4", [B, 4, D], F32, kind="Internal")
        turned, copied = k.once("l0_turned", 2 * G16), k.once("l0_copied", 2 * G16)
        g_done, g_copied, g_out, g_in = (k.once(n, c) for n, c in (("g_done", 1), ("g_copied", 1), ("g_out", 32), ("g_in", 16)))
        corr_done, v_steps, exped = k.once("corr_done", 1), k.once("l0_v_steps", 13 + 2 * TOP - 1), k.once("l0_exped", 1)
        made, mixed_done, mixed_copied = k.once("l0_made", 2), k.once("mixed_done", 1), k.once("mixed_copied", 1)
        rows_done, rows_ready, rows_out, loaded2 = k.once("rows_done", 1), k.once("rows4_ready", 1), k.once("rows_out", 16 * 4), k.once("weights", 16 * 2)
        rows_in = k.once("rows_in", 16 * 32)
        step = [0]
        with nc.Block() as block:
            @block.sync
            def _(sp):
                sp.dma_start(wout[:, :, :], io["L0_xattn_Wout"].rearrange("(c t) d -> t c d", t=S))\
                    .then_inc(loaded2.sem, 16)
                sp.dma_start(bout[:, :], row_on_all(io["L0_xattn_bout"], D))\
                    .then_inc(loaded2.sem, 16)
                sp.wait_ge(*g_copied.now(0))
                for n in range(2):
                    sp.dma_start(g_dram[n * S:(n + 1) * S, :], g_sb[0:S, :]).then_inc(g_out.sem, 16)
                sp.wait_ge(*g_out.now(0))
                sp.dma_start(diag[:, :], bass.AP(tensor=g_dram, offset=0, ap=[[S + 1, S], [S, S]]),
                             allow_slow_non_contiguous=True).then_inc(g_in.sem, 16)
                sp.wait_ge(*rows_ready.now(0))
                for n in range(4):
                    b2, half = n // 2, n % 2
                    sp.dma_start(bass.AP(tensor=r_dram, offset=(half * 64 + b2) * 4 * D,
                                         ap=[[8 * D, 32], [D, 4], [1, D]]), rows4[:, n, :])\
                        .then_inc(rows_out.sem, 16)
                sp.wait_ge(*rows_out.now(0))
                for b2 in range(2):
                    for h in range(16):
                        lo = b2 * S + 4 * h
                        sp.dma_start(k.delta[lo:lo + 4, :, :],
                                     bass.AP(tensor=r_dram, offset=b2 * 4 * D,
                                             ap=[[D, 4], [8 * D, TILES], [1, D]])).then_inc(rows_in.sem, 16)
                sp.wait_ge(*rows_in.now(0))

            @block.gpsimd
            def _(g):
                g.iota(lag_i[:, :], pattern=[[1, P]], base=S, channel_multiplier=-1).then_inc(made.sem, 1)
                g.memset(mean[:, :], 1.0 / (B * C8)).then_inc(made.sem, 1)

            @block.tensor
            def _(pe):
                n = 0
                for g in range(G16):
                    for what in "kq":
                        if n >= 2:
                            pe.wait_ge(*copied.now(0, n - 1))
                        pe.transpose(bank_n[n % 2][:, 0:P],
                                     nat[what][:, 16 * g:16 * g + 16, :].rearrange("p t c -> p (t c)"),
                                     k.ident[:, :]).then_inc(turned.sem, 1)
                        n += 1
                pe.wait_ge(*copied.now(0))
                for g in range(G16):
                    for b in range(2):
                        cols = slice(b * S, (b + 1) * S)
                        last = pe.matmul(bank8[0:S, 0:S], gt["q"][:, g, cols], gt["k"][:, g, cols],
                                         start=(g + b == 0), stop=(g == G16 - 1 and b == 1))
                last.then_inc(g_done.sem, 1)
                pe.wait_ge(*g_in.now(0))
                pe.wait_ge(*made.now(0))
                pe.matmul(bank_z[:, 0:S], mean[:, :], diag[:, :], start=True, stop=True).then_inc(corr_done.sem, 1)
                pe.wait_ge(*loaded2.now(0))
                pe.wait_ge(*v_steps.now(0))
                for c in range(2):
                    last = pe.matmul(bank_n[0][:, c * D:(c + 1) * D], circ[:, :], wout[:, c, :],
                                     start=True, stop=True)
                last.then_inc(mixed_done.sem, 1)
                pe.wait_ge(*mixed_copied.now(0))
                for b in range(2):
                    rows = slice(b * S, (b + 1) * S)
                    for half in range(2):
                        out = bank_n[1 - b][:, half * D:(half + 1) * D]
                        for c in range(2):
                            last = pe.matmul(out, nat["k"][rows, 32 * half:32 * half + 32, c::2], mixed[rows, c, :],
                                             start=(c == 0), stop=(c == 1))
                last.then_inc(rows_done.sem, 1)

            @block.scalar
            def _(a):
                n = 0
                for g in range(G16):
                    for what in "kq":
                        a.wait_ge(*turned.now(0, n + 1))
                        a.activation(gt[what][:, g, :], bank_n[n % 2][:, 0:P], ACT.Identity).then_inc(copied.sem, 1)
                        n += 1
                a.wait_ge(*v_steps.now(0, 7))
                a.activation(wts[:, :], best[:, 0:TOP], ACT.Exp, bias=first[:, 0:1]).then_inc(exped.sem, 1)
                a.wait_ge(*mixed_done.now(0))
                a.activation(mixed[:, :, :], bank_n[0][:, 0:2 * D].rearrange("p (c d) -> p c d", c=2), ACT.Identity)\
                    .then_inc(mixed_copied.sem, 1)

            @block.vector
            def _(v):
                def done(ins):
                    ins.then_inc(v_steps.sem, 1)
                    step[0] += 1
                    v.wait_ge(*v_steps.now(0, step[0]))
                v.wait_ge(*g_done.now(0))
                v.tensor_copy(g_sb[0:S, :], bank8[0:S, 0:S]).then_inc(g_copied.sem, 1)
                v.wait_ge(*corr_done.now(0))
                done(v.tensor_copy(corr[:, :], bank_z[:, 0:S]))
                done(v.max(best[:, 0:8], corr[:, :]))
                done(v.max_index(at[:, 0:8], best[:, 0:8], corr[:, :]))
                done(v.match_replace(rest[:, :], best[:, 0:8], corr[:, :], -HUGE))
                done(v.max(best[:, 8:16], rest[:, :]))
                done(v.max_index(at[:, 8:16], best[:, 8:16], rest[:, :]))
                done(v.tensor_scalar(first[:, :], best[:, 0:1], -1.0, None, ALU.mult))
                done(v.tensor_copy(atf[:, :], at[:, :]))
                v.wait_ge(*exped.now(0))
                done(v.tensor_reduce(wsum[:, :], wts[:, :], AX.X, ALU.add))
                done(v.reciprocal(wrec[:, :], wsum[:, :]))
                done(v.tensor_scalar(wts[:, :], wts[:, :], wrec[:, 0:1], None, ALU.mult))
                v.wait_ge(*made.now(0))
                done(v.tensor_scalar(lag_i[:, :], lag_i[:, :], S - 1, None, ALU.bitwise_and))
                done(v.tensor_copy(lag[:, :], lag_i[:, :]))
                for n in range(TOP):
                    dst = part if n else circ
                    done(v.tensor_scalar(dst[:, :], lag[:, :], atf[0:S, n:n + 1], wts[0:S, n:n + 1],
                                         ALU.is_equal, ALU.mult))
                    if n:
                        done(v.tensor_tensor(circ[:, :], circ[:, :], part[:, :], ALU.add))
                v.wait_ge(*rows_done.now(0))
                for b in range(2):
                    v.tensor_tensor(rows4[:, 2 * b:2 * b + 2, :],
                                    bank_n[1 - b][:, 0:2 * D].rearrange("p (n d) -> p n d", n=2),
                                    bout[:, :].unsqueeze(1).broadcast_to([P, 2, D]), ALU.add)\
                        .then_inc(rows_summed.sem, 1)
                v.wait_ge(*rows_summed.now(0))
                v.tensor_scalar(rows4[:, :, :], rows4[:, :, :], k.gate[:, 0:1], None, ALU.mult)\
                    .then_inc(rows_ready.sem, 1)


def gather_slots(k, io):
    nc = k.nc
    H, DK, SL = 16, 8, 16
    W = 64 + 1
    with ExitStack() as ctx:
        m = Scope(nc, ctx, "l0g")
        wq, wk, wv, wo = (m.sb(n, [P, P]) for n in ("wq", "wk", "wv", "wo"))
        bq, bv, bo = m.sb("bq", [P, 1]), m.sb("bv", [P, P]), m.sb("bo", [P, P])
        slot = m.sb("slot", [P, D])
        slot_b = m.sb("slot_b", [P, D])
        slotT = m.sb("slotT", [P, SL])
        qT = m.sb("qT", [P, SL])
        q_by_head = m.sb("q_by_head", [P, H, SL])
        wkT = m.sb("wkT", [P, P])
        w_eff = m.sb("w_eff", [P, 2, P])
        sel = m.sb("sel", [P, 2 * SL])
        bank_z, bank_v = m.banks("bank_z")[0], m.banks("bank_v")[0]
        s_banks, pt_banks, o_banks = m.banks("s", 2), m.banks("pt", 2), m.banks("o", 2)
        norm = Norm(k, m, bank_z)
        top = m.sb("top", [P, 2, NB])
        pr = m.sb("pr", [P, 2, RT])
        pT = m.sb("pT", [P, 2, T, P])
        v2 = m.sb("v2", [P, T, 2, 2, W])
        rec = m.sb("rec", [P, 4])
        rm = m.sb("rm", [P, 4, 8])
        om = m.sb("om", [P, 2, 4, 64])
        fold = m.sb("fold", [P, 2, P])
        oT = m.sb("oT", [P, T, 2, SL])
        sg = k.counter
        added_first = sg("x_summed")
        scored, topped, shifted, exped = sg("scored"), sg("topped"), sg("shifted"), sg("exped")
        turned, pT_ready, v_done, v_ready = sg("p_turned"), sg("pT_ready"), sg("v_done"), sg("v_ready")
        attended, rec_ready, rm_ready, om_ready = sg("attended", T), sg("rec_ready", T), sg("rm_ready", T), sg("om_ready", T)
        fold_steps, fold_ready, f_turned, oT_ready = sg("fold_steps", T), sg("fold_ready"), sg("f_turned"), sg("oT_ready")
        projected, slots_ready = sg("projected"), sg("slots_ready")
        w_eff_ready = k.once("w_eff_ready")
        loaded, prep_pe, prep_dve, cleared = k.once("weights", 16 * 15), k.once("prep_pe", 4), k.once("prep_dve", 7), k.once("cleared", 2)
        block = ctx.enter_context(nc.Block())

        @block.sync
        def _(sp):
            n = "L0_ffn_"
            for dst, src in ((wq, "d_Wq"), (wk, "d_Wk"), (wv, "d_Wv"), (wo, "d_Wo")):
                sp.dma_start(dst[:, :], io[n + src]).then_inc(loaded.sem, 16)
            sp.dma_start(bq[:, :], column(io[n + "d_bq"]), allow_slow_non_contiguous=True).then_inc(loaded.sem, 16)
            sp.dma_start(bv[:, :], row_on_all(io[n + "d_bv"], D)).then_inc(loaded.sem, 16)
            sp.dma_start(bo[:, :], row_on_all(io[n + "d_bo"], D)).then_inc(loaded.sem, 16)
            for b in range(NB):
                sp.dma_start(slot[b * SL:(b + 1) * SL, :], io[n + "slot_query"][0]).then_inc(loaded.sem, 16)

        @block.gpsimd
        def _(g):
            opens(g, norm.eps_added, norm.rstd)
            g.memset(v2[:, :, :, :, :], 0.0).then_inc(cleared.sem, 1)
            g.wait_ge(*cleared.now(0, 1))
            g.memset(v2[0:S, :, :, 0, 64], 1.0)
            g.memset(v2[S:P, :, :, 1, 64], 1.0).then_inc(cleared.sem, 1)
            every_round(g, lambda r, p: norm.pool(g, r, p), nothing)

        @block.vector
        def _(v):
            opens(v, added_first, *norm.opened_by_vector(), topped, shifted, v_ready, rec_ready, rm_ready,
                  om_ready, slots_ready)
            v.wait_ge(*loaded.now(0))
            v.tensor_tensor(slot_b[:, :], slot[:, :], bo[:, :], ALU.add).then_inc(prep_dve.sem, 1)
            v.tensor_reduce(sel[:, 0:SL], k.ident[:, :].rearrange("p (h s) -> p s h", s=SL), AX.X, ALU.add)\
                .then_inc(prep_dve.sem, 1)
            v.memset(sel[:, SL:2 * SL], 0.0).then_inc(prep_dve.sem, 1)
            v.wait_ge(*prep_pe.now(0, 1))
            v.tensor_copy(slotT[:, :], bank_v[:, 0:SL]).then_inc(prep_dve.sem, 1)
            v.wait_ge(*prep_pe.now(0, 2))
            v.tensor_scalar(qT[:, :], s_banks[0][:, 0:SL], bq[:, 0:1], DK ** -0.5, ALU.add, ALU.mult)\
                .then_inc(prep_dve.sem, 1)
            v.wait_ge(*prep_pe.now(0, 3))
            v.tensor_copy(wkT[:, :], pt_banks[0][:, 0:P]).then_inc(prep_dve.sem, 1)
            v.wait_ge(*prep_dve.now(0, 6))
            v.tensor_tensor(q_by_head[:, :, :], qT[:, :].unsqueeze(1).broadcast_to([P, H, SL]),
                            k.by8[:, :].unsqueeze(2).broadcast_to([P, H, SL]), ALU.mult).then_inc(prep_dve.sem, 1)
            v.wait_ge(*cleared.now(0))

            def front(r, p):
                xr = k.x[:, bass.ds(r * T, T), :]
                v.tensor_tensor(xr, xr, k.delta[:, bass.ds(r * T, T), :], ALU.add).then_inc(added_first.sem, 1)
                v.wait_ge(*added_first.now(r))
                k.paced(v)
                norm.vector(v, r, p)

            def values(r, p):
                v.wait_ge(*v_done.now(r))
                v.wait_ge(*attended.ago(r, 1))
                for b in range(2):
                    rows = slice(b * S, (b + 1) * S)
                    last = v.tensor_tensor(
                        v2[rows, :, :, b, 0:64], bank_v[rows, :].rearrange("p (t g d) -> p t g d", t=T, g=2),
                        bv[rows, :].rearrange("p (g d) -> p g d", g=2).unsqueeze(1).broadcast_to([S, T, 2, 64]),
                        ALU.add)
                last.then_inc(v_ready.sem, 1)

            def main(r, p, next_values, next_front):
                v.wait_ge(*scored.now(r))
                for g in range(2):
                    last = v.tensor_reduce(top[:, g, :], s_banks[g][:, :].rearrange("p (b s) -> p b s", b=NB),
                                           AX.X, ALU.max)
                last.then_inc(topped.sem, 1)
                v.wait_ge(*topped.now(r))
                v.wait_ge(*turned.ago(r, 1))
                for g in range(2):
                    last = v.tensor_tensor(pr[:, g, :].rearrange("p (b s) -> p b s", b=NB),
                                           s_banks[g][:, :].rearrange("p (b s) -> p b s", b=NB),
                                           top[:, g, :].unsqueeze(2).broadcast_to([P, NB, S]), ALU.subtract)
                last.then_inc(shifted.sem, 1)
                next_front()
                for t in range(T):
                    o = o_banks[t % 2][:, 0:4 * W].rearrange("p (g w) -> p g w", w=W)
                    v.wait_ge(*attended.now(r, t + 1))
                    v.reciprocal(rec[:, :], o[:, :, 64]).then_inc(rec_ready.sem, 1)
                    v.wait_ge(*rec_ready.now(r, t + 1))
                    v.tensor_tensor(rm[:, :, :], k.by16[:, :].unsqueeze(1).broadcast_to([P, 4, 8]),
                                    rec[:, :].unsqueeze(2).broadcast_to([P, 4, 8]), ALU.mult).then_inc(rm_ready.sem, 1)
                    v.wait_ge(*rm_ready.now(r, t + 1))
                    if t < 2:
                        v.wait_ge(*fold_steps.ago(r, 1))
                    else:
                        v.wait_ge(*fold_steps.now(r, t - 1))
                    v.tensor_tensor(om[:, t % 2, :, :].rearrange("p g (h d) -> p g h d", h=8),
                                    o[:, :, 0:64].rearrange("p g (h d) -> p g h d", h=8),
                                    rm[:, :, :].unsqueeze(3).broadcast_to([P, 4, 8, DK]), ALU.mult)\
                        .then_inc(om_ready.sem, 1)
                next_values()
                v.wait_ge(*projected.now(r))
                v.tensor_tensor(k.slots[:, r, :], pt_banks[0][:, 0:D], slot_b[:, :], ALU.add)\
                    .then_inc(slots_ready.sem, 1)
            staggered(v, front, values, main)

        @block.scalar
        def _(a):
            opens(a, norm.ready, exped, pT_ready, fold_ready, oT_ready)
            a.wait_ge(*prep_pe.now(0))
            a.activation(w_eff[:, :, :], o_banks[0][:, 0:2 * P].rearrange("p (g c) -> p g c", g=2), ACT.Identity)\
                .then_inc(w_eff_ready.sem, 1)

            def main(r, p):
                a.wait_ge(*shifted.now(r))
                a.activation(pr[:, :, :], pr[:, :, :], ACT.Exp).then_inc(exped.sem, 1)
                a.wait_ge(*turned.now(r))
                a.wait_ge(*attended.ago(r, 1))
                for g in range(2):
                    last = a.activation(pT[:, g, :, :], pt_banks[g][:, :].rearrange("p (t c) -> p t c", t=T), ACT.Identity)
                last.then_inc(pT_ready.sem, 1)
                a.wait_ge(*fold_steps.now(r))
                a.activation(fold[:, :, :].rearrange("p b (g d) -> p g b d", g=2),
                             pt_banks[0][:, 0:2 * P].rearrange("p (g b d) -> p g b d", g=2, b=2), ACT.Identity)\
                    .then_inc(fold_ready.sem, 1)
                a.wait_ge(*f_turned.now(r))
                a.activation(oT[:, :, :, :].rearrange("p t b s -> p b t s"),
                             pt_banks[1][:, 0:2 * P].rearrange("p (b t s) -> p b t s", b=2, t=T)[:, :, :, 0:SL],
                             ACT.Identity).then_inc(oT_ready.sem, 1)
            every_round(a, lambda r, p: norm.scalar(a, r, p, v_done, scored), main)

        @block.tensor
        def _(pe):
            opens(pe, norm.turned, scored, turned, v_done, attended, fold_steps, f_turned, projected)
            pe.wait_ge(*loaded.now(0))
            pe.transpose(bank_v[:, 0:SL], slot[0:SL, :], k.ident[0:SL, 0:SL]).then_inc(prep_pe.sem, 1)
            pe.wait_ge(*prep_dve.now(0, 4))
            pe.matmul(s_banks[0][:, 0:SL], wq[:, :], slotT[:, :], start=True, stop=True).then_inc(prep_pe.sem, 1)
            pe.transpose(pt_banks[0][:, 0:P], wk[:, :], k.ident[:, :]).then_inc(prep_pe.sem, 1)
            pe.wait_ge(*prep_dve.now(0))
            pe.matmul(o_banks[0][:, 0:2 * P], wkT[:, :], q_by_head[:, :, :].rearrange("p h s -> p (h s)"),
                      start=True, stop=True).then_inc(prep_pe.sem, 1)
            pe.wait_ge(*w_eff_ready.now(0))

            def front(r, p):
                norm.tensor(pe, r, p)
                pe.wait_ge(*norm.ready.now(r))
                pe.wait_ge(*v_ready.ago(r, 1))
                for t in range(T):
                    last = pe.matmul(bank_v[:, t * P:(t + 1) * P], norm.zT[p][:, t * P:(t + 1) * P], wv[:, :],
                                     start=True, stop=True)
                last.then_inc(v_done.sem, 1)
                pe.wait_ge(*shifted.ago(r, 1))
                for g in range(2):
                    last = pe.matmul(s_banks[g][:, :], w_eff[:, g, :], norm.zT[p][:, :], start=True, stop=True)
                last.then_inc(scored.sem, 1)

            def main(r, p):
                pe.wait_ge(*slots_ready.ago(r, 1))
                pe.wait_ge(*oT_ready.ago(r, 1))
                pe.wait_ge(*pT_ready.ago(r, 1))
                pe.wait_ge(*exped.now(r))
                for g in range(2):
                    for t in range(T):
                        last = pe.transpose(pt_banks[g][:, t * P:(t + 1) * P], pr[:, g, t * P:(t + 1) * P], k.ident[:, :])
                last.then_inc(turned.sem, 1)
                pe.wait_ge(*pT_ready.now(r))
                pe.wait_ge(*v_ready.now(r))
                for t in range(T):
                    if t < 2:
                        pe.wait_ge(*om_ready.ago(r, 1))
                    else:
                        pe.wait_ge(*om_ready.now(r, t - 1))
                    for g in range(2):
                        last = pe.matmul(o_banks[t % 2][:, g * 2 * W:(g + 1) * 2 * W], pT[:, g, t, :],
                                         v2[:, t, g, :, :].rearrange("p b w -> p (b w)"), start=True, stop=True)
                    last.then_inc(attended.sem, 1)
                    if t:
                        fold_heads(r, t - 1)
                fold_heads(r, T - 1)
                pe.wait_ge(*fold_ready.now(r))
                for b in range(2):
                    last = pe.transpose(pt_banks[1][:, b * P:(b + 1) * P], fold[:, b, :], k.ident[:, :])
                last.then_inc(f_turned.sem, 1)
                pe.wait_ge(*oT_ready.now(r))
                pe.matmul(pt_banks[0][:, 0:D], oT[:, :, :, :].rearrange("p t b s -> p (t b s)"), wo[:, :],
                          start=True, stop=True).then_inc(projected.sem, 1)

            def fold_heads(r, t):
                pe.wait_ge(*om_ready.now(r, t + 1))
                mm = pe.matmul(pt_banks[0][32 * t:32 * t + 32, 0:256], sel[:, :],
                               om[:, t % 2, :, :].rearrange("p g d -> p (g d)"), start=True, stop=True)
                mm.then_inc(fold_steps.sem, 1)
            every_round(pe, front, main)


def experts(k, io):
    nc = k.nc
    E, F = 16, 512
    C = F // P
    with ExitStack() as ctx:
        m = Scope(nc, ctx, "l0e")
        ln_g, ln_b = m.sb("ln_g", [P, D]), m.sb("ln_b", [P, D])
        b1_raw, bg_raw, b2_raw = m.sb("b1_raw", [E, F]), m.sb("bg_raw", [E, F]), m.sb("b2_raw", [E, D])
        b1, bg, b2 = m.sb("b1", [P, E, C]), m.sb("bg", [P, E, C]), m.sb("b2", [P, E])
        st, mv = m.sb("st", [P, ROUNDS, 6]), m.sb("mv", [P, ROUNDS, 2])
        ve, rs = m.sb("ve", [P, ROUNDS]), m.sb("rs", [P, ROUNDS])
        h = m.sb("h", [P, ROUNDS, D])
        hT = m.sb("hT", [P, E, B])
        w1, wg = ([m.sb(f"{n}{p}", [P, F]) for p in range(2)] for n in ("w1", "wg"))
        w2 = [m.sb(f"w2{p}", [P, C, D]) for p in range(2)]
        u, gt, ug = ([m.sb(f"{n}{p}", [P, C, B]) for p in range(2)] for n in ("u", "gt", "ug"))
        banks = m.banks("bank_t", 2)
        u_banks, g_banks, y_banks = m.banks("bank_u", 2), m.banks("bank_g", 2), m.banks("bank_y", 2)
        loaded, w_in = k.once("weights", 16 * (2 * NB + 3)), [k.semaphore(f"up_in{p}") for p in range(2)]
        w2_in = [k.semaphore(f"down_in{p}") for p in range(2)]
        b_turned, b_ready = k.once("b_turned", 3), k.once("b_ready", 3)
        n_steps, rstd = k.once("n_steps", 3 * ROUNDS + 2), k.once("slot_rstd", 2)
        s_turned, s_copied = k.once("s_turned", 8), k.once("s_copied", 8)
        summed = k.once("b2_summed", 1)
        sg = k.counter
        up_done, biased_up, silu_done, gated = sg("up_done"), sg("biased_up", 2), sg("silu_done", 2), sg("gated_up")
        down_done, slot_added = sg("down_done"), sg("slot_added")
        block = ctx.enter_context(nc.Block())

        def up_in(e, p):
            return w_in[p], e * 16 + (32 - 16 * p)

        def down_in(e, p):
            return w2_in[p], e * 8 + (16 - 8 * p)

        @block.sync
        def _(sp):
            n = "L0_ffn_"
            for b in range(NB):
                sp.dma_start(ln_g[b * E:(b + 1) * E, :], io[n + "e_ln_g"]).then_inc(loaded.sem, 16)
                sp.dma_start(ln_b[b * E:(b + 1) * E, :], io[n + "e_ln_b"]).then_inc(loaded.sem, 16)
            for dst, src in ((b1_raw, "e_b1"), (bg_raw, "e_bg"), (b2_raw, "e_b2")):
                sp.dma_start(dst[:, :], io[n + src]).then_inc(loaded.sem, 16)

            def load(e, p):
                sp.wait_ge(*up_done.ago(e, 2))
                sp.dma_start(w1[p][:, :], io[n + "e_W1"][e]).then_inc(w_in[p], 16)
                sp.dma_start(wg[p][:, :], io[n + "e_Wg"][e]).then_inc(w_in[p], 16)
                sp.wait_ge(*down_done.ago(e, 2))
                sp.dma_start(w2[p][:, :, :], io[n + "e_W2"][e].rearrange("(c p) n -> p c n", p=P)).then_inc(w2_in[p], 16)
            every_round(sp, nothing, load)

        @block.gpsimd
        def _(g):
            g.wait_ge(*n_steps.now(0, 2 * ROUNDS))
            g.tensor_tensor(ve[:, :], mv[:, :, 1], k.eps[:, :], ALU.add).then_inc(rstd.sem, 1)
            g.wait_ge(*rstd.now(0, 1))
            g.tensor_tensor(rs[:, :], ve[:, :], k.minus_half[:, :], ALU.pow).then_inc(rstd.sem, 1)

        @block.vector
        def _(v):
            opens(v, biased_up, gated, slot_added)
            for r in range(ROUNDS):
                v.bn_stats(st[:, r, :], k.slots[:, r, :]).then_inc(n_steps.sem, 1)
            v.wait_ge(*n_steps.now(0, ROUNDS))
            for r in range(ROUNDS):
                v.bn_aggr(mv[:, r, :], st[:, r, :]).then_inc(n_steps.sem, 1)
            v.wait_ge(*rstd.now(0))
            v.wait_ge(*n_steps.now(0, 2 * ROUNDS))
            for r in range(ROUNDS):
                v.tensor_scalar(h[:, r, :], k.slots[:, r, :], mv[:, r, 0:1], rs[:, r:r + 1], ALU.subtract,
                                ALU.mult).then_inc(n_steps.sem, 1)
            v.wait_ge(*loaded.now(0))
            v.wait_ge(*n_steps.now(0, 3 * ROUNDS))
            v.tensor_tensor(h[:, :, :], h[:, :, :], ln_g[:, :].unsqueeze(1).broadcast_to([P, ROUNDS, D]), ALU.mult)\
                .then_inc(n_steps.sem, 1)
            v.wait_ge(*n_steps.now(0, 3 * ROUNDS + 1))
            v.tensor_tensor(h[:, :, :], h[:, :, :], ln_b[:, :].unsqueeze(1).broadcast_to([P, ROUNDS, D]), ALU.add)\
                .then_inc(n_steps.sem, 1)
            v.wait_ge(*s_copied.now(0))
            v.wait_ge(*b_ready.now(0))
            v.tensor_tensor(k.oT[:, :, :], k.oT[:, :, :], b2[:, :].unsqueeze(2).broadcast_to([P, E, B]), ALU.add)\
                .then_inc(summed.sem, 1)
            v.wait_ge(*summed.now(0))

            def main(e, p):
                v.wait_ge(*up_done.now(e))
                v.wait_ge(*gated.ago(e, 2))
                for dst, bank, bias in ((u, u_banks, b1), (gt, g_banks, bg)):
                    v.tensor_tensor(dst[p][:, :, :], bank[p][:, :].rearrange("p (c b) -> p c b", c=C),
                                    bias[:, e, :].unsqueeze(2).broadcast_to([P, C, B]), ALU.add)\
                        .then_inc(biased_up.sem, 1)
                v.wait_ge(*silu_done.now(e))
                v.wait_ge(*down_done.ago(e, 2))
                v.tensor_tensor(ug[p][:, :, :], u[p][:, :, :], gt[p][:, :, :], ALU.mult).then_inc(gated.sem, 1)
                v.wait_ge(*down_done.now(e))
                v.tensor_tensor(k.oT[:, e, :], k.oT[:, e, :], y_banks[p][:, 0:B], ALU.add).then_inc(slot_added.sem, 1)
            every_round(v, nothing, main)

        @block.scalar
        def _(a):
            opens(a, silu_done)
            load_table(k, a, ACT.Silu)
            a.wait_ge(*b_turned.now(0))
            a.activation(b1[:, :, :].rearrange("p e c -> p c e"), u_banks[0][:, 0:C * E].rearrange("p (c e) -> p c e", c=C), ACT.Identity).then_inc(b_ready.sem, 1)
            a.activation(bg[:, :, :].rearrange("p e c -> p c e"), g_banks[0][:, 0:C * E].rearrange("p (c e) -> p c e", c=C), ACT.Identity).then_inc(b_ready.sem, 1)
            a.activation(b2[:, :], y_banks[0][:, 0:E], ACT.Identity).then_inc(b_ready.sem, 1)
            for n in range(8):
                q = n // 2
                dst = (k.oT, hT)[n % 2]
                a.wait_ge(*s_turned.now(0, n + 1))
                a.activation(dst[:, :, 32 * q:32 * q + 32].rearrange("p e (g b) -> p g b e", g=4),
                             banks[n % 2][:, :].rearrange("p (g b e) -> p g b e", g=4, b=NB), ACT.Identity)\
                    .then_inc(s_copied.sem, 1)

            def main(e, p):
                for n, buf in enumerate((u, gt)):
                    a.wait_ge(*biased_up.now(e, n + 1))
                    a.activation(buf[p][:, :, :], buf[p][:, :, :], ACT.Silu).then_inc(silu_done.sem, 1)
            every_round(a, nothing, main)

        @block.tensor
        def _(pe):
            opens(pe, up_done, down_done)
            pe.wait_ge(*loaded.now(0))
            for raw, bank in ((b1_raw, u_banks[0]), (bg_raw, g_banks[0])):
                for c in range(C):
                    last = pe.transpose(bank[:, c * E:(c + 1) * E], raw[:, c * P:(c + 1) * P], k.ident[0:E, 0:E])
                last.then_inc(b_turned.sem, 1)
            pe.transpose(y_banks[0][:, 0:E], b2_raw[:, :], k.ident[0:E, 0:E]).then_inc(b_turned.sem, 1)
            for n in range(8):
                q = n // 2
                src = (k.slots, h)[n % 2]
                if n == 1:
                    pe.wait_ge(*n_steps.now(0))
                if n >= 2:
                    pe.wait_ge(*s_copied.now(0, n - 1))
                for g in range(4):
                    last = pe.transpose(banks[n % 2][:, g * P:(g + 1) * P], src[:, 4 * q + g, :], k.ident[:, :])
                last.then_inc(s_turned.sem, 1)
            pe.wait_ge(*s_copied.now(0))
            pe.wait_ge(*b_ready.now(0))

            def up(e, p):
                pe.wait_ge(*up_in(e, p))
                pe.wait_ge(*biased_up.ago(e, 2))
                for w, bank in ((w1, u_banks), (wg, g_banks)):
                    for c in range(C):
                        last = pe.matmul(bank[p][:, c * B:(c + 1) * B], w[p][:, c * P:(c + 1) * P], hT[:, e, :],
                                         start=True, stop=True)
                last.then_inc(up_done.sem, 1)

            def down(e, p):
                pe.wait_ge(*down_in(e, p))
                pe.wait_ge(*gated.now(e))
                pe.wait_ge(*slot_added.ago(e, 2))
                for c in range(C):
                    last = pe.matmul(y_banks[p][:, 0:B], w2[p][:, c, :], ug[p][:, c, :], start=(c == 0), stop=(c == C - 1))
                last.then_inc(down_done.sem, 1)
            every_round(pe, up, down)


def read_slots(k, io):
    nc = k.nc
    H, DK, SL = 16, 8, 16
    with ExitStack() as ctx:
        m = Scope(nc, ctx, "l0r")
        wq, wk, wv, wo = (m.sb(n, [P, P]) for n in ("wq", "wk", "wv", "wo"))
        bq, bq_s, bk, bv = (m.sb(n, [P, 1]) for n in ("bq", "bq_s", "bk", "bv"))
        bo, bo_gated = m.sb("bo", [P, D]), m.sb("bo_gated", [P, D])
        bank_z, bank_p, bank_k, bank_o = (m.banks("bank_" + n)[0] for n in "zpko")
        s_banks, pt_banks = m.banks("s", 2), m.banks("pt", 2)
        norm = Norm(k, m, bank_z)
        qT = m.sb("qT", [P, RT])
        sl = m.sb("sl", [P, NB, SL])
        kT = m.sb("kT", [P, NB, SL])
        kb = [m.sb(f"kb{p}", [P, NB, H, SL]) for p in range(2)]
        top, total, rec = (m.sb(n, [P, T, H]) for n in ("top", "total", "rec"))
        pr = m.sb("pr", [P, T, H, SL])
        pn = m.sb("pn", [P, T, H, SL])
        aT = m.sb("aT", [P, T, 2, P])
        sl_rep = m.sb("sl_rep", [P, NB, 8, SL])
        vb = [m.sb(f"vb{p}", [P, NB, D]) for p in range(2)]
        oT = m.sb("oT", [P, RT])
        sg = k.counter
        q_done, qT_ready, sl_ready, k_done, kT_ready, kb_ready = (sg(n) for n in ("q_done", "qT_ready", "sl_ready", "k_done", "kT_ready", "kb_ready"))
        scored, topped, shifted, exped, summed, rec_ready, probs = (sg(n) for n in ("scored", "topped", "shifted", "exped", "summed", "rec_ready", "probs"))
        turned, aT_ready, rep_ready, v_done, vb_ready = sg("p_turned"), sg("aT_ready"), sg("rep_ready"), sg("v_done", 2), sg("vb_ready", 2)
        attended, oT_ready, projected, biased, added = (sg(n) for n in ("attended", "oT_ready", "projected", "biased", "added"))
        loaded, prep = k.once("weights", 16 * 8), k.once("prep_dve", 2)
        block = ctx.enter_context(nc.Block())

        @block.sync
        def _(sp):
            n = "L0_ffn_c_"
            for dst, src in ((wq, "Wq"), (wk, "Wk"), (wv, "Wv"), (wo, "Wo")):
                sp.dma_start(dst[:, :], io[n + src]).then_inc(loaded.sem, 16)
            for dst, src in ((bq, "bq"), (bk, "bk"), (bv, "bv")):
                sp.dma_start(dst[:, :], column(io[n + src]), allow_slow_non_contiguous=True).then_inc(loaded.sem, 16)
            sp.dma_start(bo[:, :], row_on_all(io[n + "bo"], D)).then_inc(loaded.sem, 16)

        @block.gpsimd
        def _(g):
            opens(g, norm.eps_added, norm.rstd, biased, sl_ready, kb_ready)
            g.wait_ge(*prep.now(0))

            def norm_front(r, p):
                g.wait_ge(*k_done.ago(r, 1))
                g.wait_ge(*rep_ready.ago(r, 1))
                k.paced(g)
                g.tensor_copy(sl[:, :, :].rearrange("p b s -> p s b"), k.oT[:, :, bass.ds(r * NB, NB)])\
                    .then_inc(sl_ready.sem, 1)
                norm.pool(g, r, p)

            def front(r, p):
                g.wait_ge(*scored.ago(r, 2))
                g.wait_ge(*kT_ready.now(r))
                for b in range(NB):
                    last = g.tensor_tensor(kb[p][:, b, :, :], kT[:, b, :].unsqueeze(1).broadcast_to([P, H, SL]),
                                           k.by8[:, :].unsqueeze(2).broadcast_to([P, H, SL]), ALU.mult)
                last.then_inc(kb_ready.sem, 1)

            def main(r, p, next_front, next_norm):
                next_front()
                g.wait_ge(*norm.normed.now(r))
                k.paced(g)
                xr = k.x[:, bass.ds(r * T, T), :]
                g.tensor_tensor(xr, xr, bo_gated[:, :].unsqueeze(1).broadcast_to([P, T, D]), ALU.add)\
                    .then_inc(biased.sem, 1)
                next_norm()
            staggered(g, norm_front, front, main)

        @block.vector
        def _(v):
            opens(v, *norm.opened_by_vector(), topped, shifted, summed, rec_ready, probs, vb_ready, added)
            v.wait_ge(*loaded.now(0))
            v.tensor_scalar(bo_gated[:, :], bo[:, :], k.gate[:, 4:5], None, ALU.mult).then_inc(prep.sem, 1)
            v.tensor_scalar(bq_s[:, :], bq[:, :], DK ** -0.5, None, ALU.mult).then_inc(prep.sem, 1)

            def values(r, p):
                for g in range(2):
                    v.wait_ge(*attended.ago(r, 2))
                    v.wait_ge(*v_done.now(r, g + 1))
                    v.tensor_tensor(vb[p][:, 4 * g:4 * g + 4, :].rearrange("p b (g h d) -> p (b g) h d", g=2, h=8),
                                    bank_k[:, :].rearrange("p (b h d) -> p b h d", b=8, h=8),
                                    k.by16[:, :].unsqueeze(1).unsqueeze(3).broadcast_to([P, 8, 8, DK]), ALU.mult)\
                        .then_inc(vb_ready.sem, 1)

            def softmax_start(r, p):
                v.wait_ge(*scored.now(r))
                for g in range(2):
                    last = v.tensor_reduce(top[:, 2 * g:2 * g + 2, :],
                                           s_banks[g][:, :].rearrange("p (t h s) -> p t h s", t=2, h=H), AX.X, ALU.max)
                last.then_inc(topped.sem, 1)
                v.wait_ge(*topped.now(r))
                v.wait_ge(*probs.ago(r, 1))
                for g in range(2):
                    last = v.tensor_tensor(pr[:, 2 * g:2 * g + 2, :, :].rearrange("p t h s -> p (t h) s"),
                                           s_banks[g][:, :].rearrange("p (h s) -> p h s", s=SL),
                                           top[:, 2 * g:2 * g + 2, :].rearrange("p t h -> p (t h)").unsqueeze(2)
                                           .broadcast_to([P, 2 * H, SL]), ALU.subtract)
                last.then_inc(shifted.sem, 1)

            def front(r, p, step=None):
                if step != "softmax":
                    values(r, p)
                if step != "values":
                    softmax_start(r, p)

            def main(r, p, next_front, next_norm):
                next_front("values")
                v.wait_ge(*exped.now(r))
                v.tensor_reduce(total[:, :, :], pr[:, :, :, :], AX.X, ALU.add).then_inc(summed.sem, 1)
                v.wait_ge(*summed.now(r))
                v.reciprocal(rec[:, :, :], total[:, :, :]).then_inc(rec_ready.sem, 1)
                v.wait_ge(*turned.ago(r, 1))
                v.wait_ge(*rec_ready.now(r))
                v.tensor_tensor(pn[:, :, :, :].rearrange("p t h s -> p (t h) s"),
                                pr[:, :, :, :].rearrange("p t h s -> p (t h) s"),
                                rec[:, :, :].rearrange("p t h -> p (t h)").unsqueeze(2).broadcast_to([P, T * H, SL]),
                                ALU.mult).then_inc(probs.sem, 1)
                next_norm()
                next_front("softmax")
                v.wait_ge(*projected.now(r))
                v.wait_ge(*biased.now(r))
                xr = k.x[:, bass.ds(r * T, T), :]
                v.scalar_tensor_tensor(xr, bank_p[:, :].rearrange("p (t d) -> p t d", t=T),
                                       k.gate[:, 4:5], xr, ALU.mult, ALU.add).then_inc(added.sem, 1)
            staggered(v, lambda r, p: norm.vector(v, r, p), front, main)

        @block.scalar
        def _(a):
            opens(a, norm.ready, rep_ready, qT_ready, kT_ready, exped, aT_ready, oT_ready)
            load_table(k, a, ACT.Exp)
            a.wait_ge(*prep.now(0))

            def front(r, p):
                a.wait_ge(*v_done.ago(r, 1))
                a.wait_ge(*sl_ready.now(r))
                a.activation(sl_rep[:, :, :, :], sl[:, :, :].unsqueeze(2).broadcast_to([P, NB, 8, SL]),
                             ACT.Identity).then_inc(rep_ready.sem, 1)
                a.wait_ge(*kb_ready.ago(r, 1))
                a.wait_ge(*k_done.now(r))
                a.activation(kT[:, :, :], bank_k[:, 0:P].rearrange("p (b s) -> p b s", b=NB), ACT.Identity,
                             bias=bk[:, 0:1]).then_inc(kT_ready.sem, 1)
                norm.scalar(a, r, p, q_done)
                a.wait_ge(*scored.ago(r, 1))
                a.wait_ge(*q_done.now(r))
                a.activation(qT[:, :], bank_p[:, :], ACT.Identity, bias=bq_s[:, 0:1], scale=DK ** -0.5)\
                    .then_inc(qT_ready.sem, 1)

            def main(r, p, next_front):
                next_front()
                a.wait_ge(*shifted.now(r))
                a.activation(pr[:, :, :, :], pr[:, :, :, :], ACT.Exp).then_inc(exped.sem, 1)
                a.wait_ge(*turned.now(r))
                a.wait_ge(*attended.ago(r, 1))
                for g in range(2):
                    last = a.activation(aT[:, 2 * g:2 * g + 2, :, :],
                                        pt_banks[g][:, :].rearrange("p (t g q) -> p t g q", t=2, g=2), ACT.Identity)
                last.then_inc(aT_ready.sem, 1)
                a.wait_ge(*attended.now(r))
                a.activation(oT[:, :], bank_o[:, :], ACT.Identity, bias=bv[:, 0:1]).then_inc(oT_ready.sem, 1)
            next_round_within(a, front, main)

        @block.tensor
        def _(pe):
            opens(pe, norm.turned, q_done, k_done, scored, turned, v_done, attended, projected)
            pe.wait_ge(*loaded.now(0))

            def front(r, p):
                pe.wait_ge(*vb_ready.ago(r, 1))
                pe.wait_ge(*sl_ready.now(r))
                pe.matmul(bank_k[:, 0:P], wk[:, :], sl[:, :, :].rearrange("p b s -> p (b s)"), start=True, stop=True)\
                    .then_inc(k_done.sem, 1)
                norm.tensor(pe, r, p)
                pe.wait_ge(*added.ago(r, 2))
                pe.wait_ge(*norm.ready.now(r))
                pe.matmul(bank_p[:, :], wq[:, :], norm.zT[p][:, :], start=True, stop=True).then_inc(q_done.sem, 1)
                pe.wait_ge(*rep_ready.now(r))
                for g in range(2):
                    pe.wait_ge(*(vb_ready.now(r, 1) if g else kT_ready.now(r)))
                    for b in range(4):
                        last = pe.matmul(bank_k[:, b * D:(b + 1) * D],
                                         sl_rep[:, 4 * g + b, :, :].rearrange("p h s -> p (h s)"), wv[:, :],
                                         start=True, stop=True)
                    last.then_inc(v_done.sem, 1)
                pe.wait_ge(*qT_ready.now(r))
                pe.wait_ge(*shifted.ago(r, 1))
                pe.wait_ge(*kb_ready.now(r))
                for b in range(NB):
                    t = b // 2
                    last = pe.matmul(s_banks[t // 2][b % 2 * S:b % 2 * S + S, t % 2 * 256:t % 2 * 256 + 256],
                                     qT[:, b * S:(b + 1) * S], kb[p][:, b, :, :].rearrange("p h s -> p (h s)"),
                                     start=True, stop=True)
                last.then_inc(scored.sem, 1)

            def main(r, p):
                pe.wait_ge(*aT_ready.ago(r, 1))
                pe.wait_ge(*probs.now(r))
                for t in range(T):
                    for g in range(2):
                        n = t % 2 * 2 + g
                        last = pe.transpose(pt_banks[t // 2][:, n * P:(n + 1) * P],
                                            pn[:, t, 8 * g:8 * g + 8, :].rearrange("p h s -> p (h s)"), k.ident[:, :])
                last.then_inc(turned.sem, 1)
                pe.wait_ge(*oT_ready.ago(r, 1))
                pe.wait_ge(*vb_ready.now(r))
                pe.wait_ge(*aT_ready.now(r))
                for b in range(NB):
                    for g in range(2):
                        last = pe.matmul(bank_o[g * 64:(g + 1) * 64, b * S:(b + 1) * S],
                                         vb[p][:, b, g * 64:(g + 1) * 64], aT[:, b // 2, g, b % 2 * S:b % 2 * S + S],
                                         start=True, stop=True)
                last.then_inc(attended.sem, 1)
                pe.wait_ge(*added.ago(r, 1))
                pe.wait_ge(*oT_ready.now(r))
                for t in range(T):
                    last = pe.matmul(bank_p[:, t * D:(t + 1) * D], oT[:, t * P:(t + 1) * P], wo[:, :],
                                     start=True, stop=True)
                last.then_inc(projected.sem, 1)
            every_round(pe, front, main)


def slot_ffn(k, io):
    with ExitStack() as ctx:
        m = Scope(k.nc, ctx, "l0s")
        k.slots = m.sb("slots", [P, ROUNDS, D])
        k.oT = m.sb("oT", [P, 16, B])
        gather_slots(k, io)
        experts(k, io)
        read_slots(k, io)


def first_layer(k, io):
    with ExitStack() as ctx:
        k.delta = Scope(k.nc, ctx, "l0").sb("delta", [P, TILES, D])
        correlation_attention(k, io)
        slot_ffn(k, io)


def turned_weight(pe, a, k, raw, bank, dst, turned, copied, n):
    if pe is not None:
        if n:
            pe.wait_ge(*copied.now(0, n))
        pe.transpose(bank[:, 0:P], raw, k.ident[:, :]).then_inc(turned.sem, 1)
    if a is not None:
        a.wait_ge(*turned.now(0, n + 1))
        a.activation(dst, bank[:, 0:P], ACT.Identity).then_inc(copied.sem, 1)


def relative_attention(k, io):
    nc = k.nc
    H, DK = 16, 8
    HP = H // 2
    N2 = 2 * (DK + 1)
    KB = 4
    with ExitStack() as ctx:
        m = Scope(nc, ctx, "l1x")
        NREL = 511
        table = m.sb("table", [P, 4, H])
        table_T = m.sb("table_T", [H, 512])
        USED = 2 * S - 1
        FIRST = NREL // 2 - (S - 1)
        by_head = nc.dram_tensor("rel_by_query", [S + 1, H, 256], F32, kind="Internal")
        table_done, table_turned = k.once("table_done", 1), k.once("table_turned", 1)
        table_out, bias_in = k.once("table_out", 16), k.once("bias_in", 32)
        raw = m.sb("raw", [P, 4, P])
        w = m.sb("w", [P, 4, P])
        fc_b = m.sb("fc_b", [P, D])
        fc_b_gated = m.sb("fc_b_gated", [P, D])
        bias = m.sb("bias", [P, H, S])
        bank_z = m.banks("bank_z")[0]
        bank_p = m.banks("bank_p")[0]
        bank_v = m.banks("bank_v")[0]
        s_banks = m.banks("scores", 2)
        pt_banks = m.banks("pt", 2)
        bank_o = m.banks("bank_o")[0]
        norm = Norm(k, m, bank_z)
        qT = [m.sb(f"qT{p}", [P, RT]) for p in range(2)]
        kT = [m.sb(f"kT{p}", [P, RT]) for p in range(2)]
        cT = m.sb("cT", [P, RT])
        v2 = [m.sb(f"v2_{p}", [P, NB, HP, N2]) for p in range(2)]
        kb = [m.sb(f"kb{i}", [P, H, S]) for i in range(KB)]
        sc = m.sb("sc", [P, H, S])
        top = m.sb("top", [P, H])
        pr = [m.sb(f"pr{i}", [P, H, S]) for i in range(2)]
        pT = m.sb("pT", [P, HP, P])
        rec = m.sb("rec", [P, H])
        on = m.sb("on", [P, T, D])
        oT = m.sb("oT", [P, RT])
        sg = k.counter
        qk_done, qT_ready, kT_ready = sg("qk_done", 2), sg("qT_ready"), sg("kT_ready")
        c_copied, v_done, v_ready = sg("c_copied"), sg("v_done", 2), sg("v_ready", 4)
        kb_ready, scored, shifted_in = sg("kb_ready", NB), sg("scored", NB), sg("biased_scores", T)
        topped, shifted, exped = sg("topped", T), sg("shifted", T), sg("exped", T)
        p_turned, pT_ready, attended = sg("p_turned", T), sg("pT_ready", T), sg("attended", T)
        rec_ready, on_ready, o_turned, oT_ready = sg("rec_ready", T), sg("on_ready", T), sg("o_turned"), sg("oT_ready")
        projected, biased, added = sg("projected"), sg("biased"), sg("added")
        loaded = k.once("weights", 16 * 7)
        turned, copied = k.once("w_turned", 4), k.once("w_copied", 4)
        prep, cleared = k.once("prep_dve", 1), k.once("v2_cleared", 6)
        block = ctx.enter_context(nc.Block())
        srcs = ["L1_xattn_wq", "L1_xattn_wk", "L1_xattn_wv", "L1_xattn_fc_w"]

        @block.sync
        def _(sp):
            for n, name in enumerate(srcs):
                sp.dma_start(raw[:, n, :], io[name]).then_inc(loaded.sem, 16)
            sp.dma_start(fc_b[:, :], row_on_all(io["L1_xattn_fc_b"], D)).then_inc(loaded.sem, 16)
            rel = io["L1_xattn_rel_table"]
            sp.dma_start(table[:, 0:3, :], rel[0:3 * P, :].rearrange("(c p) h -> p c h", p=P)).then_inc(loaded.sem, 16)
            sp.dma_start(table[0:P - 1, 3, :], rel[3 * P:NREL, :]).then_inc(loaded.sem, 16)
            sp.wait_ge(*table_turned.now(0))
            sp.dma_start(bass.AP(tensor=by_head, offset=0, ap=[[256, H], [H * 256 + 1, S], [1, USED]]),
                         table_T[:, FIRST:FIRST + USED].unsqueeze(1).broadcast_to([H, S, USED]))\
                .then_inc(table_out.sem, 16)
            sp.wait_ge(*table_out.now(0))
            for b in range(2):
                sp.dma_start(bias[b * S:(b + 1) * S, :, :],
                             bass.AP(tensor=by_head, offset=S - 1, ap=[[H * 256, S], [256, H], [1, S]]))\
                    .then_inc(bias_in.sem, 16)

        @block.gpsimd
        def _(g):
            opens(g, norm.eps_added, norm.rstd, biased, kb_ready)
            for v in v2:
                g.memset(v[:, :, :, :], 0.0).then_inc(cleared.sem, 1)
            g.wait_ge(*cleared.now(0, 2))
            for v in v2:
                g.memset(v[0:S, :, :, DK], 1.0).then_inc(cleared.sem, 1)
                g.memset(v[S:P, :, :, 2 * DK + 1], 1.0).then_inc(cleared.sem, 1)
            g.wait_ge(*prep.now(0))

            def main(r, p):
                g.wait_ge(*kT_ready.now(r))
                for b in range(NB):
                    g.wait_ge(*(scored.now(r, b - KB + 1) if b >= KB else scored.ago(r, 1, NB + b - KB + 1)))
                    g.tensor_tensor(kb[b % KB][:, :, :],
                                    kT[p][:, b * S:(b + 1) * S].unsqueeze(1).broadcast_to([P, H, S]),
                                    k.by8[:, :].unsqueeze(2).broadcast_to([P, H, S]), ALU.mult)\
                        .then_inc(kb_ready.sem, 1)
                g.wait_ge(*norm.normed.now(r))
                k.paced(g)
                xr = k.x[:, bass.ds(r * T, T), :]
                g.tensor_tensor(xr, xr, fc_b_gated[:, :].unsqueeze(1).broadcast_to([P, T, D]), ALU.add)\
                    .then_inc(biased.sem, 1)
            every_round(g, lambda r, p: norm.pool(g, r, p), main)

        @block.vector
        def _(v):
            opens(v, *norm.opened_by_vector(), shifted_in, topped, shifted, rec_ready, on_ready, added)
            v.wait_ge(*loaded.now(0))
            v.tensor_scalar(fc_b_gated[:, :], fc_b[:, :], k.gate[:, 1:2], None, ALU.mult).then_inc(prep.sem, 1)
            v.wait_ge(*cleared.now(0))
            v.wait_ge(*bias_in.now(0))

            def scores(r, t):
                v.wait_ge(*(shifted.now(r, t) if t else shifted.ago(r, 1)))
                v.wait_ge(*scored.now(r, 2 * t + 2))
                for half in range(2):
                    last = v.tensor_tensor(sc[:, 8 * half:8 * half + 8, :],
                                           s_banks[half][:, :].rearrange("p (h s) -> p h s", h=8),
                                           bias[:, 8 * half:8 * half + 8, :], ALU.add)
                last.then_inc(shifted_in.sem, 1)
                v.wait_ge(*shifted_in.now(r, t + 1))
                v.tensor_reduce(top[:, :], sc[:, :, :], AX.X, ALU.max).then_inc(topped.sem, 1)
                v.wait_ge(*topped.now(r, t + 1))
                v.wait_ge(*(p_turned.now(r, t - 1) if t >= 2 else p_turned.ago(r, 1, T + t - 1)))
                v.tensor_tensor(pr[t % 2][:, :, :], sc[:, :, :],
                                top[:, :].unsqueeze(2).broadcast_to([P, H, S]), ALU.subtract)\
                    .then_inc(shifted.sem, 1)

            def norm_out(r, t):
                o = bank_o[:, 0:H * (DK + 1)].rearrange("p (h d) -> p h d", h=H)
                v.wait_ge(*attended.now(r, t + 1))
                v.reciprocal(rec[:, :], o[:, :, DK]).then_inc(rec_ready.sem, 1)
                if t == 0:
                    v.wait_ge(*o_turned.ago(r, 1))
                v.wait_ge(*rec_ready.now(r, t + 1))
                v.tensor_tensor(on[:, t, :].rearrange("p (h d) -> p h d", h=H), o[:, :, 0:DK],
                                rec[:, :].unsqueeze(2).broadcast_to([P, H, DK]), ALU.mult)\
                    .then_inc(on_ready.sem, 1)

            def main(r, p, next_front):
                for t in range(T):
                    scores(r, t)
                    if t >= 2:
                        norm_out(r, t - 2)
                norm_out(r, T - 2)
                next_front()
                norm_out(r, T - 1)
                v.wait_ge(*projected.now(r))
                v.wait_ge(*biased.now(r))
                xr = k.x[:, bass.ds(r * T, T), :]
                v.scalar_tensor_tensor(xr, bank_v[:, :].rearrange("p (t d) -> p t d", t=T),
                                       k.gate[:, 1:2], xr, ALU.mult, ALU.add).then_inc(added.sem, 1)
            every_round_within(v, lambda r, p: norm.vector(v, r, p), main)

        @block.scalar
        def _(a):
            a.wait_ge(*cleared.now(0))
            opens(a, norm.ready, c_copied, qT_ready, kT_ready, v_ready, exped, pT_ready, oT_ready)
            a.wait_ge(*table_done.now(0))
            a.activation(table_T[:, 0:NREL], bank_v[0:H, 0:NREL], ACT.Identity).then_inc(table_turned.sem, 1)
            for n in range(4):
                turned_weight(None, a, k, raw[:, n, :], bank_p, w[:, n, :], turned, copied, n)

            def front(r, p):
                a.wait_ge(*v_done.ago(r, 1))
                k.paced(a)
                a.activation(cT[:, :], k.cT[:, bass.ds(r * RT, RT)], ACT.Identity).then_inc(c_copied.sem, 1)
                norm.scalar(a, r, p, qk_done)
                a.wait_ge(*qk_done.now(r, 1))
                a.wait_ge(*scored.ago(r, 2))
                a.activation(qT[p][:, :], bank_p[:, :], ACT.Identity, scale=DK ** -0.5).then_inc(qT_ready.sem, 1)
                values(r, p, 0)
                a.wait_ge(*qk_done.now(r, 2))
                a.wait_ge(*kb_ready.ago(r, 2))
                a.activation(kT[p][:, :], bank_p[:, :], ACT.Identity).then_inc(kT_ready.sem, 1)
                values(r, p, 1)

            def values(r, p, g):
                a.wait_ge(*attended.ago(r, 2))
                a.wait_ge(*v_done.now(r, g + 1))
                for h2 in range(2):
                    rows = slice(h2 * S, (h2 + 1) * S)
                    a.activation(
                        v2[p][rows, 4 * g:4 * g + 4, :, h2 * (DK + 1):h2 * (DK + 1) + DK],
                        bank_v[rows, :].rearrange("p (b g h d) -> p b g h d", b=4, g=HP, h=2)[:, :, :, h2, :],
                        ACT.Identity).then_inc(v_ready.sem, 1)

            def main(r, p, next_front):
                next_front()
                for t in range(T):
                    a.wait_ge(*shifted.now(r, t + 1))
                    a.activation(pr[t % 2][:, :, :], pr[t % 2][:, :, :], ACT.Exp).then_inc(exped.sem, 1)
                    a.wait_ge(*(attended.now(r, t) if t else attended.ago(r, 1)))
                    a.wait_ge(*p_turned.now(r, t + 1))
                    for half in range(2):
                        last = a.activation(pT[:, 4 * half:4 * half + 4, :],
                                            pt_banks[half][:, :].rearrange("p (g q) -> p g q", g=4), ACT.Identity)
                    last.then_inc(pT_ready.sem, 1)
                a.wait_ge(*o_turned.now(r))
                a.activation(oT[:, :], bank_p[:, :], ACT.Identity).then_inc(oT_ready.sem, 1)
            next_round_within(a, front, main)

        @block.tensor
        def _(pe):
            opens(pe, norm.turned, qk_done, v_done, scored, p_turned, attended, o_turned, projected)
            pe.wait_ge(*loaded.now(0))
            for c in range(4):
                rows = P if c < 3 else P - 1
                last = pe.transpose(bank_v[0:H, c * P:c * P + rows], table[0:rows, c, :], k.ident[0:rows, 0:rows])
            last.then_inc(table_done.sem, 1)
            for n in range(4):
                turned_weight(pe, None, k, raw[:, n, :], bank_p, w[:, n, :], turned, copied, n)
            pe.wait_ge(*copied.now(0))

            def front(r, p):
                norm.tensor(pe, r, p)
                pe.wait_ge(*norm.ready.now(r))
                pe.matmul(bank_p[:, :], w[:, 0, :], norm.zT[p][:, :], start=True, stop=True)\
                    .then_inc(qk_done.sem, 1)
                pe.wait_ge(*added.ago(r, 2))
                pe.wait_ge(*c_copied.now(r))
                values(r, 0)
                pe.wait_ge(*qT_ready.now(r))
                pe.matmul(bank_p[:, :], w[:, 1, :], cT[:, :], start=True, stop=True).then_inc(qk_done.sem, 1)
                pe.wait_ge(*v_ready.now(r, 2))
                values(r, 1)
                pe.wait_ge(*kT_ready.now(r))
                pe.wait_ge(*v_ready.now(r))

            def values(r, g):
                for b in range(4):
                    for h2 in range(2):
                        last = pe.matmul(bank_v[h2 * S:(h2 + 1) * S, b * D:(b + 1) * D],
                                         cT[:, (4 * g + b) * S:(4 * g + b + 1) * S], w[:, 2, :],
                                         start=True, stop=True)
                last.then_inc(v_done.sem, 1)

            def scores(r, p, t):
                for b in (2 * t, 2 * t + 1):
                    if b % 2 == 0:
                        pe.wait_ge(*(shifted_in.now(r, t) if t else shifted_in.ago(r, 1)))
                    pe.wait_ge(*kb_ready.now(r, b + 1))
                    rows = slice(b % 2 * S, b % 2 * S + S)
                    for half in range(2):
                        last = pe.matmul(s_banks[half][rows, :], qT[p][:, b * S:(b + 1) * S],
                                         kb[b % KB][:, 8 * half:8 * half + 8, :].rearrange("p h s -> p (h s)"),
                                         start=True, stop=True)
                    last.then_inc(scored.sem, 1)

            def turn(r, t):
                pe.wait_ge(*(pT_ready.now(r, t) if t else pT_ready.ago(r, 1)))
                pe.wait_ge(*exped.now(r, t + 1))
                for g in range(HP):
                    last = pe.transpose(pt_banks[g // 4][:, g % 4 * P:(g % 4 + 1) * P],
                                        pr[t % 2][:, 2 * g:2 * g + 2, :].rearrange("p h s -> p (h s)"),
                                        k.ident[:, :])
                last.then_inc(p_turned.sem, 1)

            def attend(r, p, t):
                pe.wait_ge(*(on_ready.now(r, t) if t else on_ready.ago(r, 1)))
                pe.wait_ge(*pT_ready.now(r, t + 1))
                for b in range(2):
                    for g in range(HP):
                        last = pe.matmul(bank_o[b * S:(b + 1) * S, g * N2:(g + 1) * N2],
                                         pT[:, g, b * S:(b + 1) * S], v2[p][:, 2 * t + b, g, :],
                                         start=True, stop=True)
                last.then_inc(attended.sem, 1)

            def main(r, p, next_front):
                scores(r, p, 0)
                next_front()
                for t in range(T):
                    if t + 1 < T:
                        scores(r, p, t + 1)
                    if t:
                        attend(r, p, t - 1)
                    turn(r, t)
                attend(r, p, T - 1)
                pe.wait_ge(*on_ready.now(r))
                for t in range(T):
                    last = pe.transpose(bank_p[:, t * P:(t + 1) * P], on[:, t, :], k.ident[:, :])
                last.then_inc(o_turned.sem, 1)
                pe.wait_ge(*added.ago(r, 1))
                pe.wait_ge(*oT_ready.now(r))
                for t in range(T):
                    last = pe.matmul(bank_v[:, t * D:(t + 1) * D], oT[:, t * P:(t + 1) * P], w[:, 3, :],
                                     start=True, stop=True)
                last.then_inc(projected.sem, 1)
            next_round_within(pe, front, main)


def feed_forward(k, io, tag, gate, func, experts):
    nc = k.nc
    H = 512
    C = H // P
    E = len(experts["w1"])
    routed = experts.get("routed", False)
    HB = 3
    with ExitStack() as ctx:
        m = Scope(nc, ctx, tag)
        w1 = [m.sb(f"w1_{e}", [P, H]) for e in range(E)]
        w2 = [m.sb(f"w2_{e}", [P, C, D]) for e in range(E)]
        b1 = m.sb("b1", [P, E, C])
        b2 = m.sb("b2", [P, E, D])
        b2_sum = m.sb("b2_sum", [P, D])
        b2_gated = m.sb("b2_gated", [P, D])
        gw = m.sb("gw", [P, 2])
        gd = m.sb("gd", [P, 1])
        low = {}
        if "low_rank" in experts:
            R = 32
            low = dict(u1=m.sb("u1", [P, R]), u1T=m.sb("u1T", [R, P]), v1=m.sb("v1", [R, H]),
                       u2=m.sb("u2", [P, C, R]), u2T=m.sb("u2T", [R, C, P]), v2=m.sb("v2", [R, D]))
        bank_z = m.banks("bank_z")[0]
        hidden_banks = m.banks("hidden", HB)
        out_bank = m.banks("out", 2)
        gate_bank = m.banks("gate")[0]
        norm = Norm(k, m, bank_z)
        ze = [[m.sb(f"ze{p}_{e}", [P, RT]) for e in range(2)] for p in range(2)] if routed else None
        N = E * C
        hid = [m.sb(f"hid{i}", [P, RT]) for i in range(HB)]
        sg = k.counter
        if routed:
            gates, routed_in = sg("gate_scores"), sg("routed", 2)
        hidden, activated, projected = sg("hidden", N), sg("activated", N), sg("projected", N)
        biased, added = sg("biased"), sg("added")
        loads = experts["loads"](io, dict(w1=w1, w2=w2, b1=b1, b2=b2, gw=gw, **low))
        loaded = k.once("weights", 16 * len(loads))
        prep_pe, prep_act = (k.once(n, 7 if low else 0) for n in ("prep_pe", "prep_act"))
        prep_dve = k.once("prep_dve", E + 1 + routed)
        block = ctx.enter_context(nc.Block())

        def z_of(e, p):
            return ze[p][e] if routed and e < 2 else norm.zT[p]

        @block.sync
        def _(sp):
            for dst, src in loads:
                sp.dma_start(dst, src, allow_slow_non_contiguous=True).then_inc(loaded.sem, 16)

        @block.vector
        def _(v):
            opens(v, *norm.opened_by_vector(), *((routed_in,) if routed else ()), added)
            v.wait_ge(*loaded.now(0))
            v.tensor_copy(b2_sum[:, :], b2[:, 0, :]).then_inc(prep_dve.sem, 1)
            step = 1
            for e in range(1, E):
                v.wait_ge(*prep_dve.now(0, step))
                v.tensor_tensor(b2_sum[:, :], b2_sum[:, :], b2[:, e, :], ALU.add).then_inc(prep_dve.sem, 1)
                step += 1
            v.wait_ge(*prep_dve.now(0, step))
            v.tensor_scalar(b2_gated[:, :], b2_sum[:, :], k.gate[:, gate:gate + 1], None, ALU.mult)\
                .then_inc(prep_dve.sem, 1)
            if routed:
                v.tensor_tensor(gd[:, :], gw[:, 1:2], gw[:, 0:1], ALU.subtract).then_inc(prep_dve.sem, 1)

            def front(r, p):
                norm.vector(v, r, p)

            def route(r, p):
                v.wait_ge(*gates.now(r))
                v.wait_ge(*norm.ready.now(r))
                v.wait_ge(*projected.ago(r, 1))
                v.scalar_tensor_tensor(ze[p][1][:, :], gate_bank[:, :], 0.0, norm.zT[p][:, :],
                                       ALU.is_gt, ALU.mult).then_inc(routed_in.sem, 1)
                v.scalar_tensor_tensor(ze[p][0][:, :], gate_bank[:, :], 0.0, norm.zT[p][:, :],
                                       ALU.is_le, ALU.mult).then_inc(routed_in.sem, 1)

            def main(r, p, next_front):
                if routed:
                    route(r, p)
                next_front()
                v.wait_ge(*projected.now(r))
                v.wait_ge(*biased.now(r))
                xr = k.x[:, bass.ds(r * T, T), :]
                v.scalar_tensor_tensor(xr, out_bank[p][:, :].rearrange("p (t d) -> p t d", t=T),
                                       k.gate[:, gate:gate + 1], xr, ALU.mult, ALU.add)\
                    .then_inc(added.sem, 1)
            every_round_within(v, front, main)

        @block.gpsimd
        def _(g):
            opens(g, norm.eps_added, norm.rstd, biased)
            g.wait_ge(*prep_dve.now(0, E + 1))

            def main(r, p):
                g.wait_ge(*norm.normed.now(r))
                k.paced(g)
                xr = k.x[:, bass.ds(r * T, T), :]
                bias = b2_gated[:, :].unsqueeze(1).broadcast_to([P, T, D])
                g.tensor_tensor(xr, xr, bias, ALU.add).then_inc(biased.sem, 1)
            every_round(g, lambda r, p: norm.pool(g, r, p), main)

        @block.scalar
        def _(a):
            opens(a, norm.ready, activated)
            if low:
                for n, dst in enumerate([low["u1T"][:, :]] + [low["u2T"][:, c, :] for c in range(C)]):
                    a.wait_ge(*prep_pe.now(0, 5))
                    a.activation(dst, hidden_banks[0][0:32, n * P:(n + 1) * P] if n < 4 else
                                 hidden_banks[1][0:32, 0:P], ACT.Identity).then_inc(prep_act.sem, 1)
                a.wait_ge(*prep_pe.now(0, 6))
                a.activation(w1[0][:, :], hidden_banks[2][:, :], ACT.Identity).then_inc(prep_act.sem, 1)
                a.wait_ge(*prep_pe.now(0, 7))
                a.activation(w2[0][:, :, :].rearrange("p c d -> p (c d)"), gate_bank[:, :], ACT.Identity)\
                    .then_inc(prep_act.sem, 1)
            a.wait_ge(*loaded.now(0))
            load_table(k, a, func)

            def front(r, p):
                if routed:
                    norm.scalar(a, r, p, projected, routed_in)
                else:
                    norm.scalar(a, r, p, projected)

            def main(r, p):
                for n in range(N):
                    e, c = n // C, n % C
                    a.wait_ge(*hidden.now(r, n + 1))
                    if n >= HB:
                        a.wait_ge(*projected.now(r, n + 1 - HB))
                    else:
                        a.wait_ge(*projected.ago(r, 1, N + n + 1 - HB))
                    a.activation(hid[n % HB][:, :], hidden_banks[n % HB][:, :], func,
                                 bias=b1[:, e, c:c + 1]).then_inc(activated.sem, 1)
            every_round(a, front, main)

        @block.tensor
        def _(pe):
            opens(pe, norm.turned, *((gates,) if routed else ()), hidden, projected)
            pe.wait_ge(*loaded.now(0))
            if low:
                pe.transpose(hidden_banks[0][0:32, 0:P], low["u1"][:, :], k.ident[:, :]).then_inc(prep_pe.sem, 1)
                for c in range(C):
                    dst = hidden_banks[0][0:32, (c + 1) * P:(c + 2) * P] if c < 3 else hidden_banks[1][0:32, 0:P]
                    pe.transpose(dst, low["u2"][:, c, :], k.ident[:, :]).then_inc(prep_pe.sem, 1)
                pe.wait_ge(*prep_act.now(0, 5))
                pe.matmul(hidden_banks[2][:, :], low["u1T"][:, :], low["v1"][:, :], start=True, stop=True)\
                    .then_inc(prep_pe.sem, 1)
                for c in range(C):
                    last = pe.matmul(gate_bank[:, c * D:(c + 1) * D], low["u2T"][:, c, :], low["v2"][:, :],
                                     start=True, stop=True)
                last.then_inc(prep_pe.sem, 1)
                pe.wait_ge(*prep_act.now(0, 7))
            if routed:
                pe.wait_ge(*prep_dve.now(0))

            def front(r, p):
                norm.tensor(pe, r, p)
                if routed:
                    pe.wait_ge(*norm.ready.now(r))
                    pe.wait_ge(*routed_in.ago(r, 1))
                    pe.matmul(gate_bank[:, :], gd[:, 0:1].broadcast_to([P, P]), norm.zT[p][:, :],
                              start=True, stop=True).then_inc(gates.sem, 1)

            def main(r, p):
                pe.wait_ge(*norm.ready.now(r))
                order = ([2, 0, 1] if routed else [0])
                for n in range(N + 2):
                    if n < N:
                        e, c = n // C, n % C
                        src = order[e]
                        if routed and e == 1 and c == 0:
                            pe.wait_ge(*routed_in.now(r))
                        if n >= HB:
                            pe.wait_ge(*activated.now(r, n + 1 - HB))
                        else:
                            pe.wait_ge(*activated.ago(r, 1, N + n + 1 - HB))
                        pe.matmul(hidden_banks[n % HB][:, :], w1[src][:, c * P:(c + 1) * P],
                                  z_of(src, p)[:, :], start=True, stop=True).then_inc(hidden.sem, 1)
                    if n >= 2:
                        o = n - 2
                        e, c = o // C, o % C
                        if o == 0:
                            pe.wait_ge(*added.ago(r, 2))
                        pe.wait_ge(*activated.now(r, o + 1))
                        for t in range(T):
                            last = pe.matmul(out_bank[p][:, t * D:(t + 1) * D],
                                             hid[o % HB][:, t * P:(t + 1) * P], w2[order[e]][:, c, :],
                                             start=(o == 0 and t == 0), stop=(o == N - 1),
                                             skip_group_check=True)
                        last.then_inc(projected.sem, 1)
            every_round(pe, front, main)


def chunked(ap):
    return ap.rearrange("(c p) n -> p c n", p=P)


def low_rank_ffn(k, io):
    def loads(io, s):
        n = "L1_ffn_"
        return [(s["u1"][:, :], io[n + "U1"]), (s["v1"][:, :], io[n + "V1"]),
                (s["u2"][:, :, :], chunked(io[n + "U2"])), (s["v2"][:, :], io[n + "V2"]),
                (s["b1"][:, 0, :], io[n + "b1"].rearrange("(c p) -> p c", p=P)),
                (s["b2"][:, 0, :], row_on_all(io[n + "b2"], D))]
    feed_forward(k, io, "l1f", 5, ACT.Gelu_apprx_tanh, dict(w1=[0], low_rank=True, loads=loads))


def routed_ffn(k, io):
    def loads(io, s):
        n = "L3_ffn_"
        out = [(s["gw"][:, :], io[n + "gate_w"].rearrange("e d -> d e"))]
        for e in range(3):
            w1 = io[n + "w1"][e] if e < 2 else io[n + "sw1"]
            w2 = io[n + "w2"][e] if e < 2 else io[n + "sw2"]
            b1 = io[n + "b1"][e] if e < 2 else io[n + "sb1"]
            out += [(s["w1"][e][:, :], w1), (s["w2"][e][:, :, :], chunked(w2)),
                    (s["b1"][:, (1, 2, 0)[e], :], b1.rearrange("(c p) -> p c", p=P)),
                    (s["b2"][:, e, :], row_on_all(io[n + ("b2" if e < 2 else "sb2")], D,
                                                  offset=e * D if e < 2 else 0))]
        return out
    feed_forward(k, io, "l3f", 7, ACT.Relu, dict(w1=[0, 1, 2], routed=True, loads=loads))


def mixing_attention(k, io):
    nc = k.nc
    H = 8
    R = 2 * S
    ROW = H * R
    SCALE = float(D) ** -0.5
    with ExitStack() as ctx:
        m = Scope(nc, ctx, "l2x")
        w = m.sb("w", [P, 4, H, P])
        u = m.sb("u", [P, H])
        mixing_weights(k, io, w, u)
        bank_z = m.banks("bank_z")[0]
        a_banks, s_banks, y_banks = m.banks("bank_a", 2), m.banks("bank_s", 2), m.banks("bank_y", 2)
        bank_pt = m.banks("bank_pt")[0]
        norm = Norm(k, m, bank_z)
        by_offset = [nc.dram_tensor(f"score_by_offset{p}", [P, T * ROW], F32, kind="Internal") for p in range(2)]
        offset_term = m.sb("offset_term", [P, T, H, R])
        pos = [m.sb(f"pos{p}", [P, T, H, S]) for p in range(2)]
        mask8 = m.sb("mask8", [P, TILES, S], mybir.dt.uint8)
        barred = [m.sb(f"barred{p}", [P, T, S]) for p in range(2)]
        pos_bias = m.sb("pos_bias", [P, H, S])
        zA = m.sb("zA", [P, H, RT])
        cz = m.sb("cz", [P, NB, 2, D])
        pr = m.sb("pr", [P, H, S])
        sc = m.sb("sc", [P, H, S])
        top, total, rec = (m.sb(n, [P, H]) for n in ("top", "total", "rec"))
        pT = m.sb("pT", [P, H // 2, P])
        yT = m.sb("yT", [P, H, 2, S])
        sg = k.counter
        bar_steps, barred_ready = sg("bar_steps"), sg("barred_ready")
        pos_done, pos_copied = sg("pos_done", 2 * T), sg("pos_copied", 2 * T)
        pos_out, pos_in, pos_barred = sg("pos_out", 16 * T), sg("pos_in", 32), sg("pos_barred", 2)
        zA_done, zA_ready, c_in = sg("zA_done", H), sg("zA_ready", H), sg("c_in", 32)
        scored, score_sum, topped, shifted = sg("scored", T), sg("biased_scores", T), sg("topped", T), sg("shifted", T)
        exped, summed, rec_ready, probs = sg("exped", T), sg("summed", T), sg("rec_ready", T), sg("probs", T)
        turned, pT_ready, attended = sg("p_turned", T), sg("pT_ready", T), sg("attended", T)
        yT_ready, projected, added = sg("oT_ready", T), sg("projected", T), sg("added")
        mask_in, cleared = k.once("mask_in", 32), k.once("cleared", 1)
        bias_out, bias_in = k.once("table_out", 16), k.once("bias_in", 32)
        block = ctx.enter_context(nc.Block())

        @block.sync
        def _(sp):
            mask = io["mask_BxS2_bf1"]
            for b in range(2):
                sp.dma_start(mask8[b * S:(b + 1) * S, :, :],
                             bass.AP(tensor=mask.tensor, offset=b * S, ap=[[0, S], [2 * S, TILES], [1, S]]))\
                    .then_inc(mask_in.sem, 16)
            sp.dma_start(by_offset[0][:, 0:ROW], w[:, 3, :, :].rearrange("p h r -> p (h r)"))\
                .then_inc(bias_out.sem, 16)
            sp.wait_ge(*bias_out.now(0))
            for b in range(2):
                sp.dma_start(pos_bias[b * S:(b + 1) * S, :, :],
                             bass.AP(tensor=by_offset[0], offset=b * S * T * ROW + S,
                                     ap=[[T * ROW - 1, S], [R, H], [1, S]])).then_inc(bias_in.sem, 16)
            sp.wait_ge(*bias_in.now(0))
            sp.sem_inc(pos_out.sem, pos_out.credit)
            sp.sem_inc(pos_in.sem, pos_in.credit)

            def skew(r, p):
                sp.wait_ge(*pos_in.ago(r, 2))
                for t in range(T):
                    sp.wait_ge(*pos_copied.now(r, 2 * t + 2))
                    sp.dma_start(by_offset[p][:, t * ROW:(t + 1) * ROW], offset_term[:, t, :, :].rearrange("p h r -> p (h r)"))\
                        .then_inc(pos_out.sem, 16)
                sp.wait_ge(*pos_out.now(r))
                sp.wait_ge(*score_sum.ago(r, 2))
                for b in range(2):
                    sp.dma_start(pos[p][b * S:(b + 1) * S, :, :, :],
                                 bass.AP(tensor=by_offset[p], offset=b * S * T * ROW + S,
                                         ap=[[T * ROW - 1, S], [R, T * H], [1, S]]))\
                        .then_inc(pos_in.sem, 16)
            every_round(sp, skew, nothing)

        @block.gpsimd
        def _(g):
            opens(g, norm.eps_added, norm.rstd, pos_barred)
            g.memset(cz[:, :, :, :], 0.0).then_inc(cleared.sem, 1)

            g.wait_ge(*bias_in.now(0))

            def front(r, p):
                norm.pool(g, r, p)
                g.wait_ge(*pos_in.now(r))
                g.tensor_tensor(pos[p][:, :, :, :].rearrange("p t h s -> p t (h s)"),
                                pos[p][:, :, :, :].rearrange("p t h s -> p t (h s)"),
                                pos_bias[:, :, :].rearrange("p h s -> p (h s)").unsqueeze(1)
                                .broadcast_to([P, T, H * S]), ALU.add).then_inc(pos_barred.sem, 1)
                g.wait_ge(*barred_ready.now(r))
                g.wait_ge(*pos_barred.now(r, 1))
                for t in range(T):
                    last = g.tensor_tensor(pos[p][:, t, :, :], pos[p][:, t, :, :],
                                           barred[p][:, t, :].unsqueeze(1).broadcast_to([P, H, S]), ALU.add)
                last.then_inc(pos_barred.sem, 1)
            every_round(g, front, nothing)

        @block.vector
        def _(v):
            opens(v, *norm.opened_by_vector(), bar_steps, barred_ready, score_sum, topped, shifted,
                  summed, rec_ready, probs, added)
            v.wait_ge(*mask_in.now(0))

            def front(r, p):
                norm.vector(v, r, p)
                v.wait_ge(*pos_barred.ago(r, 2))
                v.tensor_scalar(barred[p][:, :, :], mask8[:, bass.ds(r * T, T), :], 1.0, HUGE,
                                ALU.subtract, ALU.mult).then_inc(bar_steps.sem, 1)
                v.wait_ge(*bar_steps.now(r))
                v.tensor_scalar(barred[p][:, :, :], barred[p][:, :, :], 10.0, None, ALU.mult)\
                    .then_inc(barred_ready.sem, 1)

            def chain(r, p, t):
                v.wait_ge(*scored.now(r, t + 1))
                for b in range(2):
                    rows = slice(b * S, (b + 1) * S)
                    for g in range(2):
                        last = v.tensor_tensor(
                            sc[rows, 4 * g:4 * g + 4, :],
                            s_banks[g][rows, :].rearrange("p (h b k) -> p h b k", h=4, b=2)[:, :, b, :],
                            pos[p][rows, t, 4 * g:4 * g + 4, :], ALU.add)
                last.then_inc(score_sum.sem, 1)
                v.wait_ge(*score_sum.now(r, t + 1))
                v.tensor_reduce(top[:, :], sc[:, :, :], AX.X, ALU.max).then_inc(topped.sem, 1)
                v.wait_ge(*topped.now(r, t + 1))
                v.wait_ge(*(turned.now(r, t) if t else turned.ago(r, 1)))
                v.tensor_tensor(pr[:, :, :], sc[:, :, :], top[:, :].unsqueeze(2).broadcast_to([P, H, S]),
                                ALU.subtract).then_inc(shifted.sem, 1)
                v.wait_ge(*exped.now(r, t + 1))
                v.tensor_reduce(total[:, :], pr[:, :, :], AX.X, ALU.add).then_inc(summed.sem, 1)
                v.wait_ge(*summed.now(r, t + 1))
                v.reciprocal(rec[:, :], total[:, :]).then_inc(rec_ready.sem, 1)
                v.wait_ge(*rec_ready.now(r, t + 1))
                v.tensor_tensor(pr[:, :, :], pr[:, :, :], rec[:, :].unsqueeze(2).broadcast_to([P, H, S]),
                                ALU.mult).then_inc(probs.sem, 1)

            def main(r, p, next_front):
                v.wait_ge(*pos_barred.now(r))
                for t in range(T):
                    chain(r, p, t)
                next_front()
                v.wait_ge(*projected.now(r))
                xr = k.x[:, bass.ds(r * T, T), :]
                v.scalar_tensor_tensor(xr, a_banks[0][:, :].rearrange("p (t d) -> p t d", t=T),
                                       k.gate[:, 2:3], xr, ALU.mult, ALU.add).then_inc(added.sem, 1)
            every_round_within(v, front, main)

        @block.scalar
        def _(a):
            opens(a, norm.ready, pos_copied, zA_ready, exped, pT_ready, yT_ready)
            a.sem_inc(c_in.sem, c_in.credit)
            load_table(k, a, ACT.Exp)
            a.wait_ge(*cleared.now(0))
            by_batch = io["ctx_1024"].rearrange("b s d -> s b d")

            def front(r, p, head=None):
                if head is None:
                    position(r, p)
                    return
                if head == 0:
                    a.wait_ge(*scored.ago(r, 1))
                a.wait_ge(*zA_done.now(r, head + 1))
                a.activation(zA[:, head, :], a_banks[1][:, :], ACT.Identity, bias=u[:, head:head + 1])\
                    .then_inc(zA_ready.sem, 1)

            def position(r, p):
                norm.scalar(a, r, p, pos_done, zA_done)
                a.wait_ge(*pos_out.ago(r, 1))
                for i in range(2 * T):
                    t, half = i // 2, i % 2
                    a.wait_ge(*pos_done.now(r, i + 1))
                    a.activation(offset_term[:, t, 4 * half:4 * half + 4, :],
                                 a_banks[half][:, :].rearrange("p (h r) -> p h r", h=4), ACT.Identity)\
                        .then_inc(pos_copied.sem, 1)

            def main(r, p, next_front):
                a.wait_ge(*attended.ago(r, 1))
                k.paced(a)
                for h2 in range(2):
                    a.dma_start(cz[h2 * S:(h2 + 1) * S, :, h2, :], by_batch[:, bass.ds(r * NB, NB), :])\
                        .then_inc(c_in.sem, 16)
                next_front()
                for t in range(T):
                    a.wait_ge(*shifted.now(r, t + 1))
                    a.activation(pr[:, :, :], pr[:, :, :], ACT.Exp, scale=SCALE).then_inc(exped.sem, 1)
                    if t:
                        copy_attended(r, t - 1)
                    copy_turned(r, t)
                for h in range(4):
                    next_front(h)
                copy_attended(r, T - 1)
                for h in range(4, H):
                    next_front(h)

            def copy_turned(r, t):
                a.wait_ge(*(attended.now(r, t) if t else attended.ago(r, 1)))
                a.wait_ge(*turned.now(r, t + 1))
                a.activation(pT[:, :, :], bank_pt[:, :].rearrange("p (g q) -> p g q", q=P), ACT.Identity)\
                    .then_inc(pT_ready.sem, 1)

            def copy_attended(r, t):
                a.wait_ge(*(projected.now(r, t) if t else projected.ago(r, 1)))
                a.wait_ge(*attended.now(r, t + 1))
                for b in range(2):
                    last = a.activation(yT[:, :, b, :].rearrange("p (g h) q -> p h g q", h=2),
                                        y_banks[b][:, :].rearrange("p (h g q) -> p h g q", h=2, g=H // 2),
                                        ACT.Identity)
                last.then_inc(yT_ready.sem, 1)
            next_round_within(a, front, main, first=range(H))

        @block.tensor
        def _(pe):
            opens(pe, norm.turned, pos_done, zA_done, scored, turned, attended, projected)

            def front(r, p, head=None):
                if head is not None:
                    if head:
                        pe.wait_ge(*zA_ready.now(r, head))
                    pe.matmul(a_banks[1][:, :], w[:, 0, head, :], norm.zT[p][:, :], start=True, stop=True)\
                        .then_inc(zA_done.sem, 1)
                    return
                norm.tensor(pe, r, p)
                pe.wait_ge(*added.ago(r, 2))
                pe.wait_ge(*norm.ready.now(r))
                for i in range(2 * T):
                    t, half = i // 2, i % 2
                    if i >= 2:
                        pe.wait_ge(*pos_copied.now(r, i - 1))
                    pe.matmul(a_banks[half][:, :], norm.zT[p][:, t * P:(t + 1) * P],
                              w[:, 1, 4 * half:4 * half + 4, :].rearrange("p h r -> p (h r)"),
                              start=True, stop=True).then_inc(pos_done.sem, 1)
                pe.wait_ge(*pos_copied.now(r))

            def scores(r, t):
                pe.wait_ge(*(score_sum.now(r, t) if t else score_sum.ago(r, 1)))
                for h in range(H):
                    last = pe.matmul(s_banks[h // 4][:, h % 4 * P:(h % 4 + 1) * P], zA[:, h, t * P:(t + 1) * P],
                                     k.cT[:, bass.ds(r * RT + t * P, P)], start=True, stop=True)
                last.then_inc(scored.sem, 1)

            def turn(r, t):
                pe.wait_ge(*(pT_ready.now(r, t) if t else pT_ready.ago(r, 1)))
                pe.wait_ge(*probs.now(r, t + 1))
                for g in range(H // 2):
                    last = pe.transpose(bank_pt[:, g * P:(g + 1) * P],
                                        pr[:, 2 * g:2 * g + 2, :].rearrange("p h s -> p (h s)"), k.ident[:, :])
                last.then_inc(turned.sem, 1)

            def attend(r, t, batches=(0, 1)):
                if t == 0:
                    pe.wait_ge(*c_in.now(r))
                    pe.wait_ge(*yT_ready.ago(r, 1))
                pe.wait_ge(*pT_ready.now(r, t + 1))
                for b in batches:
                    for h2 in range(2):
                        last = pe.matmul(y_banks[b][:, h2 * 256:(h2 + 1) * 256], cz[:, 2 * t + b, h2, :],
                                         pT[:, :, b * S:(b + 1) * S], start=True, stop=True)
                if b == 1:
                    last.then_inc(attended.sem, 1)

            def project(r, t, heads=range(H)):
                pe.wait_ge(*yT_ready.now(r, t + 1))
                for h in heads:
                    last = pe.matmul(a_banks[0][:, t * D:(t + 1) * D], yT[:, h, :, :].rearrange("p b q -> p (b q)"),
                                     w[:, 2, h, :], start=(h == 0), stop=(h == H - 1))
                if h == H - 1:
                    last.then_inc(projected.sem, 1)

            def main(r, p, next_front):
                pe.wait_ge(*zA_ready.now(r))
                scores(r, 0)
                next_front()
                for t in range(T - 1):
                    scores(r, t + 1)
                    turn(r, t)
                    if t:
                        project(r, t - 1)
                    attend(r, t)
                t = T - 1
                turn(r, t)
                next_front(0)
                project(r, t - 1, range(0, 4))
                next_front(1)
                project(r, t - 1, range(4, 8))
                next_front(2)
                attend(r, t, (0,))
                next_front(3)
                attend(r, t, (1,))
                next_front(4)
                project(r, t, range(0, 4))
                next_front(5)
                project(r, t, range(4, 8))
                next_front(6)
                next_front(7)
            next_round_within(pe, front, main, first=range(H))


def mixing_weights(k, io, w, u):
    nc = k.nc
    H = 8
    with ExitStack() as ctx:
        m = Scope(nc, ctx, "l2w")
        wq, wk, wv = (m.sb(n, [P, P, H]) for n in ("wq", "wk", "wv"))
        wo = m.sb("wo", [P, H, P])
        bu, bv = m.sb("bu", [P, H]), m.sb("bv", [P, H])
        bv_wide = m.sb("bv_wide", [P, H, P])
        pos_w, posT = m.sb("pos_w", [P, P]), m.sb("posT", [P, P])
        wT = m.sb("wT", [P, 3, P])
        bank_t, bank_w, bank_u = (m.banks("bank_" + n)[0] for n in "twu")
        loaded = k.once("weights", 16 * 7)
        widened, pos_turned, posT_ready = k.once("bv_widened"), k.once("pos_turned"), k.once("posT_ready")
        turned, wT_ready = k.once("w_turned", H), k.once("w_copied", H)
        merged, w_ready, u_ready = k.once("merged", H), k.once("merged_copied", H), k.once("u_ready")
        block = ctx.enter_context(nc.Block())

        @block.sync
        def _(sp):
            n = "L2_xattn_"
            for dst, src in ((wq, "wq"), (wk, "wk"), (wv, "wv"), (wo, "wo")):
                sp.dma_start(dst[:, :, :], io[n + src]).then_inc(loaded.sem, 16)
            for dst, src in ((bu, "bu"), (bv, "bv"), (pos_w, "pos_w")):
                sp.dma_start(dst[:, :], io[n + src]).then_inc(loaded.sem, 16)

        @block.vector
        def _(v):
            v.wait_ge(*loaded.now(0))
            v.tensor_copy(bv_wide[:, :, :], bv[:, :].unsqueeze(2).broadcast_to([P, H, P])).then_inc(widened.sem, 1)
            for h in range(H):
                v.wait_ge(*merged.now(0, h + 1))
                v.tensor_copy(w[:, :, h, :], bank_w[:, :].rearrange("p (n c) -> p n c", n=4)).then_inc(w_ready.sem, 1)
            v.tensor_copy(u[:, :], bank_u[:, 0:H * H:H + 1]).then_inc(u_ready.sem, 1)
            v.wait_ge(*u_ready.now(0))

        @block.scalar
        def _(a):
            a.wait_ge(*pos_turned.now(0))
            a.activation(posT[:, :], bank_u[:, 0:P], ACT.Identity).then_inc(posT_ready.sem, 1)
            for h in range(H):
                a.wait_ge(*turned.now(0, h + 1))
                if h:
                    a.wait_ge(*merged.now(0, h))
                a.activation(wT[:, :, :], bank_t[:, 0:3 * P].rearrange("p (n c) -> p n c", n=3), ACT.Identity)\
                    .then_inc(wT_ready.sem, 1)

        @block.tensor
        def _(pe):
            pe.wait_ge(*loaded.now(0))
            pe.transpose(bank_u[:, 0:P], pos_w[:, :], k.ident[:, :]).then_inc(pos_turned.sem, 1)
            pe.wait_ge(*posT_ready.now(0))
            pe.wait_ge(*widened.now(0))
            for h in range(H):
                if h:
                    pe.wait_ge(*wT_ready.now(0, h))
                for n, raw in enumerate((wq, wk, wv)):
                    last = pe.transpose(bank_t[:, n * P:(n + 1) * P], raw[:, :, h], k.ident[:, :])
                last.then_inc(turned.sem, 1)
                pe.wait_ge(*wT_ready.now(0, h + 1))
                if h:
                    pe.wait_ge(*w_ready.now(0, h))
                for n, (left, right) in enumerate(((wT[:, 0, :], wT[:, 1, :]), (wT[:, 0, :], posT[:, :]),
                                                   (wT[:, 2, :], wo[:, h, :]), (bv_wide[:, h, :], posT[:, :]))):
                    pe.matmul(bank_w[:, n * P:(n + 1) * P], left, right, start=True, stop=True)
                pe.matmul(bank_u[:, h * H:(h + 1) * H], wT[:, 1, :], bu[:, :], start=True, stop=True)\
                    .then_inc(merged.sem, 1)


def quantized_ffn(k, io):
    nc = k.nc
    BLK = 32
    NBLK = T * D // BLK
    STEPS = 16
    MAGIC = 1.5 * 2.0 ** 23
    with ExitStack() as ctx:
        m = Scope(nc, ctx, "l2f")
        raw = m.sb("raw", [P, T, D])
        w_q = m.sb("w_q", [P, T, D])
        wT = m.sb("wT", [P, P])
        bias = m.sb("bias", [P, D])
        bias_gated = m.sb("bias_gated", [P, D])
        q_banks = m.banks("turned", 2)
        out_banks = m.banks("out", 2)
        norm = Norm(k, m, None, z_read=k.counter("quantized", STEPS))
        scratch = {n: m.sb(n, [P, NBLK, BLK]) for n in ("y", "a", "t", "u", "f", "q", "d")}
        amax, sc, inv = (m.sb(n, [P, NBLK]) for n in ("amax", "sc", "inv"))
        xd = [m.sb(f"xd{p}", [P, T, D]) for p in range(2)]
        xT = [m.sb(f"xT{p}", [P, RT]) for p in range(2)]
        sg = k.counter
        steps = norm.z_read
        turned, xT_ready, projected = sg("xd_turned"), sg("xdT_ready"), sg("projected")
        biased, added = sg("biased"), sg("added")
        loaded, w_steps = k.once("weights", 32), k.once("w_quantized", STEPS)
        prep, w_turned, w_copied = k.once("prep_dve", 2), k.once("w_turned", 1), k.once("w_copied", 1)
        block = ctx.enter_context(nc.Block())

        def quantize(v, src, dst, done, r):
            y, a, t, u, f, q, d = (scratch[n][:, :, :] for n in ("y", "a", "t", "u", "f", "q", "d"))
            src = src.rearrange("p t (b e) -> p (t b) e", e=BLK)
            dst = dst.rearrange("p t (b e) -> p (t b) e", e=BLK)

            def wide(x):
                return x[:, :].unsqueeze(2).broadcast_to([P, NBLK, BLK])
            v.tensor_reduce(amax[:, :], src, AX.X, ALU.max, apply_absolute_value=True).then_inc(done.sem, 1)
            v.wait_ge(*done.now(r, 1))
            v.tensor_scalar(sc[:, :], amax[:, :], 1 / 7.5, 1e-30, ALU.mult, ALU.max).then_inc(done.sem, 1)
            v.wait_ge(*done.now(r, 2))
            v.reciprocal(inv[:, :], sc[:, :]).then_inc(done.sem, 1)
            v.wait_ge(*done.now(r, 3))
            v.tensor_tensor(y, src, wide(inv), ALU.mult).then_inc(done.sem, 1)
            v.wait_ge(*done.now(r, 4))
            v.scalar_tensor_tensor(a, y, -1.0, y, ALU.mult, ALU.max).then_inc(done.sem, 1)
            v.wait_ge(*done.now(r, 5))
            v.tensor_scalar(t, a, 2.0, -4.0, ALU.is_ge, ALU.mult).then_inc(done.sem, 1)
            v.tensor_scalar(u, a, 4.0, -2.0, ALU.is_ge, ALU.mult).then_inc(done.sem, 1)
            v.wait_ge(*done.now(r, 7))
            v.scalar_tensor_tensor(f, t, 8.0, u, ALU.add, ALU.add).then_inc(done.sem, 1)
            v.wait_ge(*done.now(r, 8))
            v.tensor_tensor(y, y, f, ALU.mult).then_inc(done.sem, 1)
            v.wait_ge(*done.now(r, 9))
            v.tensor_scalar(q, y, MAGIC, MAGIC, ALU.add, ALU.subtract).then_inc(done.sem, 1)
            v.scalar_tensor_tensor(f, t, 0.25, u, ALU.mult, ALU.add).then_inc(done.sem, 1)
            v.wait_ge(*done.now(r, 11))
            v.tensor_tensor(d, q, y, ALU.subtract).then_inc(done.sem, 1)
            v.tensor_scalar(f, f, 0.125, 0.125, ALU.mult, ALU.subtract).then_inc(done.sem, 1)
            v.wait_ge(*done.now(r, 13))
            v.scalar_tensor_tensor(q, d, 0.5, q, ALU.is_ge, ALU.subtract).then_inc(done.sem, 1)
            v.tensor_tensor(f, f, wide(sc), ALU.mult).then_inc(done.sem, 1)
            v.wait_ge(*done.now(r, 15))
            v.tensor_tensor(dst, q, f, ALU.mult).then_inc(done.sem, 1)

        @block.sync
        def _(sp):
            sp.dma_start(raw[:, 0, :], io["L2_ffn_weight"]).then_inc(loaded.sem, 16)
            sp.dma_start(bias[:, :], row_on_all(io["L2_ffn_bias"], D)).then_inc(loaded.sem, 16)

        @block.vector
        def _(v):
            opens(v, *norm.opened_by_vector(), steps, added)
            v.memset(raw[:, 1:T, :], 0.0).then_inc(prep.sem, 1)
            v.wait_ge(*loaded.now(0))
            v.tensor_scalar(bias_gated[:, :], bias[:, :], k.gate[:, 6:7], None, ALU.mult).then_inc(prep.sem, 1)
            v.wait_ge(*prep.now(0))
            quantize(v, raw[:, :, :], w_q[:, :, :], w_steps, 0)

            def front(r, p):
                v.wait_ge(*norm.normed.now(r))
                v.wait_ge(*turned.ago(r, 2))
                quantize(v, norm.z[p][:, :, :], xd[p][:, :, :], steps, r)

            def next_norm_steps(r, p, step=None):
                if step != "finish":
                    norm.statistics(v, r, p)
                if step != "statistics":
                    norm.finish(v, r, p)

            def main(r, p, next_front, next_norm):
                next_norm("statistics")
                next_front()
                next_norm("finish")
                v.wait_ge(*projected.now(r))
                v.wait_ge(*biased.now(r))
                xr = k.x[:, bass.ds(r * T, T), :]
                v.scalar_tensor_tensor(xr, out_banks[p][:, :].rearrange("p (t d) -> p t d", t=T),
                                       k.gate[:, 6:7], xr, ALU.mult, ALU.add).then_inc(added.sem, 1)
            staggered(v, next_norm_steps, front, main)

        @block.gpsimd
        def _(g):
            opens(g, norm.eps_added, norm.rstd, biased)
            g.wait_ge(*prep.now(0))

            def main(r, p):
                g.wait_ge(*norm.normed.now(r))
                k.paced(g)
                xr = k.x[:, bass.ds(r * T, T), :]
                g.tensor_tensor(xr, xr, bias_gated[:, :].unsqueeze(1).broadcast_to([P, T, D]), ALU.add)\
                    .then_inc(biased.sem, 1)
            every_round(g, lambda r, p: norm.pool(g, r, p), main)

        @block.scalar
        def _(a):
            opens(a, xT_ready)
            a.wait_ge(*w_turned.now(0))
            a.activation(wT[:, :], q_banks[0][:, 0:P], ACT.Identity).then_inc(w_copied.sem, 1)

            def front(r, p):
                a.wait_ge(*projected.ago(r, 2))
                a.wait_ge(*turned.now(r))
                a.activation(xT[p][:, :], q_banks[p][:, :], ACT.Identity).then_inc(xT_ready.sem, 1)
            every_round(a, front, nothing)

        @block.tensor
        def _(pe):
            opens(pe, turned, projected)
            pe.wait_ge(*w_steps.now(0))
            pe.transpose(q_banks[0][:, 0:P], w_q[:, 0, :], k.ident[:, :]).then_inc(w_turned.sem, 1)
            pe.wait_ge(*w_copied.now(0))

            def main(r, p):
                pe.wait_ge(*xT_ready.ago(r, 2))
                pe.wait_ge(*steps.now(r))
                for t in range(T):
                    last = pe.transpose(q_banks[p][:, t * P:(t + 1) * P], xd[p][:, t, :], k.ident[:, :])
                last.then_inc(turned.sem, 1)
                pe.wait_ge(*added.ago(r, 2))
                pe.wait_ge(*xT_ready.now(r))
                for t in range(T):
                    last = pe.matmul(out_banks[p][:, t * D:(t + 1) * D], xT[p][:, t * P:(t + 1) * P], wT[:, :],
                                     start=True, stop=True)
                last.then_inc(projected.sem, 1)
            every_round(pe, nothing, main)


def similarity_attention(k, io):
    nc = k.nc
    with ExitStack() as ctx:
        m = Scope(nc, ctx, "l3x")
        w1_row = m.sb("w1_row", [P, D])
        b_col = m.sb("b_col", [P, 1])
        w2_col, w3_col = m.sb("w2_col", [P, 1]), m.sb("w3_col", [P, 1])
        w_qv = m.sb("w_qv", [P, 4, D])
        bias, bias_gated = m.sb("bias", [P, D]), m.sb("bias_gated", [P, D])
        bank_z, bank_s, bank_a, bank_m, bank_h, bank_b = (m.banks("bank_" + n)[0] for n in ("z", "s", "a", "m", "h", "b"))
        out_banks = m.banks("out", 2)
        weighted = k.counter("weighted", 1)
        norm = Norm(k, m, bank_z, z_read=weighted)
        zw = m.sb("zw", [P, RT])
        cs = m.sb("cs", [P, T, D])
        tmp = m.sb("tmp", [P, T, D])
        row = m.sb("row", [P, T])
        top = m.sb("top", [P, T])
        best = m.sb("best", [P, T])
        pr = m.sb("pr", [P, T, 2, S])
        total, rec = m.sb("total", [P, T]), m.sb("rec", [P, T])
        prT = m.sb("prT", [P, RT])
        bt = m.sb("bt", [T, 2, S])
        btop, bsum, brec = (m.sb(n, [T, 2]) for n in ("btop", "bsum", "brec"))
        bcol = m.sb("bcol", [P, T, 2])
        hqT, zhq, zhc = (m.sb(n, [P, RT]) for n in ("hqT", "zhq", "zhc"))
        hc = m.sb("hc", [P, NB])
        sg = k.counter
        zw_ready, c_staged = sg("zw_ready"), sg("c_staged")
        products, rows_ready = sg("row_products", 1), sg("rows_ready", 2)
        scored, topped, best_ready, shifted = sg("scored"), sg("topped"), sg("best_ready"), sg("shifted")
        exped, summed, rec_ready, probs = sg("exped"), sg("summed"), sg("rec_ready"), sg("probs")
        turned, prT_ready, hq_done, hq_ready = sg("p_turned"), sg("pT_ready"), sg("hq_done"), sg("hq_ready")
        best_turned, b_steps, b_exped, b_weights = sg("best_turned"), sg("b_steps", 5), sg("b_exped"), sg("b_weights")
        b_back, b_cols, hc_ready, zhc_ready = sg("b_back"), sg("b_cols"), sg("hc_ready"), sg("zhc_ready")
        zhq_ready, projected, biased, added = sg("zhq_ready"), sg("projected"), sg("biased"), sg("added")
        loaded, prep, cleared = k.once("weights", 16 * 6), k.once("prep_dve", 1), k.once("cleared", 2)
        block = ctx.enter_context(nc.Block())

        @block.sync
        def _(sp):
            w_sim = io["L3_xattn_w_sim"]
            sp.dma_start(w1_row[:, :], row_on_all(w_sim, D)).then_inc(loaded.sem, 16)
            sp.dma_start(w2_col[:, :], column(w_sim, offset=D), allow_slow_non_contiguous=True).then_inc(loaded.sem, 16)
            sp.dma_start(w3_col[:, :], column(w_sim, offset=2 * D), allow_slow_non_contiguous=True).then_inc(loaded.sem, 16)
            sp.dma_start(b_col[:, :], row_on_all(io["L3_xattn_b_sim"], 1)).then_inc(loaded.sem, 16)
            sp.dma_start(w_qv[:, :, :], chunked(io["L3_xattn_W_qv"])).then_inc(loaded.sem, 16)
            sp.dma_start(bias[:, :], row_on_all(io["L3_xattn_b_qv"], D)).then_inc(loaded.sem, 16)

        @block.gpsimd
        def _(g):
            opens(g, norm.eps_added, norm.rstd, biased, c_staged, products)
            g.memset(pr[:, :, :, :], 0.0).then_inc(cleared.sem, 1)
            g.memset(bcol[:, :, :], 0.0).then_inc(cleared.sem, 1)
            g.wait_ge(*prep.now(0))

            def main(r, p):
                g.wait_ge(*norm.normed.now(r))
                g.wait_ge(*rows_ready.ago(r, 1))
                g.tensor_tensor(tmp[:, :, :], norm.z[p][:, :, :],
                                w1_row[:, :].unsqueeze(1).broadcast_to([P, T, D]), ALU.mult)\
                    .then_inc(products.sem, 1)
                g.wait_ge(*hq_done.ago(r, 1))
                k.paced(g)
                g.tensor_copy(cs[:, :, :], k.c[:, bass.ds(r * T, T), :]).then_inc(c_staged.sem, 1)
                xr = k.x[:, bass.ds(r * T, T), :]
                g.tensor_tensor(xr, xr, bias_gated[:, :].unsqueeze(1).broadcast_to([P, T, D]), ALU.add)\
                    .then_inc(biased.sem, 1)
            every_round(g, lambda r, p: norm.pool(g, r, p), main)

        @block.vector
        def _(v):
            opens(v, *norm.opened_by_vector(), rows_ready, topped, best_ready, shifted, summed, rec_ready,
                  probs, b_steps, b_weights, b_cols, hc_ready, zhc_ready, zhq_ready, added)
            v.wait_ge(*loaded.now(0))
            v.tensor_scalar(bias_gated[:, :], bias[:, :], k.gate[:, 3:4], None, ALU.mult).then_inc(prep.sem, 1)
            v.wait_ge(*cleared.now(0))
            s = bank_s[:, :].rearrange("p (t b s) -> p t b s", t=T, b=2)

            def halves(fn):
                for b in range(2):
                    last = fn(slice(b * S, (b + 1) * S), b)
                return last

            def main(r, p, next_front):
                v.wait_ge(*products.now(r))
                v.tensor_reduce(row[:, :], tmp[:, :, :], AX.X, ALU.add).then_inc(rows_ready.sem, 1)
                v.wait_ge(*rows_ready.now(r, 1))
                v.tensor_scalar(row[:, :], row[:, :], b_col[:, 0:1], None, ALU.add).then_inc(rows_ready.sem, 1)
                v.wait_ge(*scored.now(r))
                halves(lambda rows, b: v.tensor_reduce(top[rows, :], s[rows, :, b, :], AX.X, ALU.max))\
                    .then_inc(topped.sem, 1)
                v.wait_ge(*topped.now(r))
                v.wait_ge(*rows_ready.now(r))
                v.wait_ge(*best_turned.ago(r, 1))
                v.tensor_tensor(best[:, :], top[:, :], row[:, :], ALU.add).then_inc(best_ready.sem, 1)
                v.wait_ge(*turned.ago(r, 1))
                halves(lambda rows, b: v.tensor_tensor(
                    pr[rows, :, b, :], s[rows, :, b, :],
                    top[rows, :].unsqueeze(2).broadcast_to([S, T, S]), ALU.subtract)).then_inc(shifted.sem, 1)
                bm = bank_m[0:T, 0:P].rearrange("p (b s) -> p b s", b=2)
                v.wait_ge(*best_turned.now(r))
                v.wait_ge(*b_back.ago(r, 1))
                v.tensor_reduce(btop[:, :], bm, AX.X, ALU.max).then_inc(b_steps.sem, 1)
                v.wait_ge(*b_steps.now(r, 1))
                v.tensor_tensor(bt[:, :, :], bm, btop[:, :].unsqueeze(2).broadcast_to([T, 2, S]), ALU.subtract)\
                    .then_inc(b_steps.sem, 1)
                v.wait_ge(*exped.now(r))
                v.tensor_reduce(total[:, :], pr[:, :, :, :].rearrange("p t b s -> p t (b s)"), AX.X, ALU.add)\
                    .then_inc(summed.sem, 1)
                v.wait_ge(*summed.now(r))
                v.reciprocal(rec[:, :], total[:, :]).then_inc(rec_ready.sem, 1)
                v.wait_ge(*rec_ready.now(r))
                halves(lambda rows, b: v.tensor_tensor(
                    pr[rows, :, b, :], pr[rows, :, b, :],
                    rec[rows, :].unsqueeze(2).broadcast_to([S, T, S]), ALU.mult)).then_inc(probs.sem, 1)
                v.wait_ge(*b_exped.now(r))
                v.tensor_reduce(bsum[:, :], bt[:, :, :], AX.X, ALU.add).then_inc(b_steps.sem, 1)
                v.wait_ge(*b_steps.now(r, 3))
                v.reciprocal(brec[:, :], bsum[:, :]).then_inc(b_steps.sem, 1)
                v.wait_ge(*b_steps.now(r, 4))
                v.tensor_tensor(bt[:, :, :], bt[:, :, :], brec[:, :].unsqueeze(2).broadcast_to([T, 2, S]), ALU.mult)\
                    .then_inc(b_steps.sem, 1)
                v.wait_ge(*b_back.now(r))
                v.wait_ge(*weighted.ago(r, 1))
                halves(lambda rows, b: v.tensor_copy(bcol[rows, :, b], bank_m[rows, P:P + T])).then_inc(b_cols.sem, 1)
                v.wait_ge(*weighted.now(r))
                v.wait_ge(*zhc_ready.ago(r, 1))
                v.tensor_copy(hc[:, :], bank_b[:, 0:NB]).then_inc(hc_ready.sem, 1)
                v.wait_ge(*hc_ready.now(r))
                v.wait_ge(*norm.ready.now(r))
                v.wait_ge(*projected.ago(r, 1))
                v.tensor_tensor(zhc[:, :].rearrange("p (b s) -> p b s", b=NB),
                                norm.zT[p][:, :].rearrange("p (b s) -> p b s", b=NB),
                                hc[:, :].unsqueeze(2).broadcast_to([P, NB, S]), ALU.mult).then_inc(zhc_ready.sem, 1)
                v.wait_ge(*hq_ready.now(r))
                v.tensor_tensor(zhq[:, :], norm.zT[p][:, :], hqT[:, :], ALU.mult).then_inc(zhq_ready.sem, 1)
                next_front()
                v.wait_ge(*projected.now(r))
                v.wait_ge(*biased.now(r))
                xr = k.x[:, bass.ds(r * T, T), :]
                v.scalar_tensor_tensor(xr, out_banks[p][:, :].rearrange("p (t d) -> p t d", t=T),
                                       k.gate[:, 3:4], xr, ALU.mult, ALU.add).then_inc(added.sem, 1)
            every_round_within(v, lambda r, p: norm.vector(v, r, p), main)

        @block.scalar
        def _(a):
            opens(a, norm.ready, zw_ready, exped, b_exped, prT_ready, hq_ready)
            a.wait_ge(*loaded.now(0))

            def main(r, p):
                a.wait_ge(*norm.ready.now(r))
                a.wait_ge(*scored.ago(r, 1))
                a.activation(zw[:, :], norm.zT[p][:, :], ACT.Identity, bias=w2_col[:, 0:1], scale=w3_col[:, 0:1])\
                    .then_inc(zw_ready.sem, 1)
                a.wait_ge(*shifted.now(r))
                for b in range(2):
                    rows = slice(b * S, (b + 1) * S)
                    last = a.activation(pr[rows, :, b, :], pr[rows, :, b, :], ACT.Exp)
                last.then_inc(exped.sem, 1)
                a.wait_ge(*b_steps.now(r, 2))
                a.activation(bt[:, :, :], bt[:, :, :], ACT.Exp).then_inc(b_exped.sem, 1)
                a.wait_ge(*hq_done.ago(r, 1))
                a.wait_ge(*turned.now(r))
                a.activation(prT[:, :], bank_a[:, :], ACT.Identity).then_inc(prT_ready.sem, 1)
                a.wait_ge(*hq_done.now(r))
                a.wait_ge(*projected.ago(r, 1))
                a.activation(hqT[:, :], bank_h[:, :], ACT.Identity).then_inc(hq_ready.sem, 1)
            every_round(a, lambda r, p: norm.scalar(a, r, p, projected), main)

        @block.tensor
        def _(pe):
            opens(pe, norm.turned, weighted, scored, turned, hq_done, best_turned, b_back, projected)
            pe.wait_ge(*loaded.now(0))

            def main(r, p):
                pe.wait_ge(*zw_ready.now(r))
                pe.wait_ge(*shifted.ago(r, 1))
                for t in range(T):
                    last = pe.matmul(bank_s[:, t * P:(t + 1) * P], zw[:, t * P:(t + 1) * P],
                                     k.cT[:, bass.ds(r * RT + t * P, P)], start=True, stop=True)
                last.then_inc(scored.sem, 1)
                pe.wait_ge(*b_cols.ago(r, 1))
                pe.wait_ge(*best_ready.now(r))
                k.paced(pe)
                pe.transpose(bank_m[0:T, 0:P], best[:, :], k.ident[:, :]).then_inc(best_turned.sem, 1)
                pe.wait_ge(*prT_ready.ago(r, 1))
                pe.wait_ge(*probs.now(r))
                for t in range(T):
                    last = pe.transpose(bank_a[:, t * P:(t + 1) * P],
                                        pr[:, t, :, :].rearrange("p b s -> p (b s)"), k.ident[:, :])
                last.then_inc(turned.sem, 1)
                pe.wait_ge(*b_steps.now(r))
                k.paced(pe)
                pe.transpose(bank_m[:, P:P + T], bt[:, :, :].rearrange("p b s -> p (b s)"), k.ident[0:T, 0:T])\
                    .then_inc(b_back.sem, 1)
                pe.wait_ge(*prT_ready.now(r))
                pe.wait_ge(*c_staged.now(r))
                pe.wait_ge(*hq_ready.ago(r, 1))
                for t in range(T):
                    last = pe.matmul(bank_h[:, t * P:(t + 1) * P], cs[:, t, :], prT[:, t * P:(t + 1) * P],
                                     start=True, stop=True)
                last.then_inc(hq_done.sem, 1)
                pe.wait_ge(*b_cols.now(r))
                pe.wait_ge(*hc_ready.ago(r, 1))
                for t in range(T):
                    last = pe.matmul(bank_b[:, 2 * t:2 * t + 2], norm.z[p][:, t, :], bcol[:, t, :],
                                     start=True, stop=True)
                last.then_inc(weighted.sem, 1)
                pe.wait_ge(*added.ago(r, 2))
                pe.wait_ge(*zhc_ready.now(r))
                pe.wait_ge(*zhq_ready.now(r))
                for t in range(T):
                    for n, part in enumerate((norm.zT[p], hqT, zhq, zhc)):
                        last = pe.matmul(out_banks[p][:, t * D:(t + 1) * D], part[:, t * P:(t + 1) * P],
                                         w_qv[:, n, :], start=(n == 0), stop=(n == 3))
                last.then_inc(projected.sem, 1)
            every_round(pe, lambda r, p: norm.tensor(pe, r, p), main)


PHASES = (first_layer, relative_attention, low_rank_ffn, mixing_attention, quantized_ffn,
          similarity_attention, routed_ffn)


def build(nc, names, args):
    io = dict(zip(names, args))
    with ExitStack() as ctx:
        k = Kit(nc, ctx)
        m = Scope(nc, ctx, "all")
        setup(k, m, io)
        turn_context(k, io)
        for phase in PHASES:
            phase(k, io)
        store(k, io)


_USED = (
    "x", "ctx_1024", "mask_BxS2_bf1", "g_xattn", "g_ffn", "L0_xattn_Wq", "L0_xattn_bq",
    "L0_xattn_Wout", "L0_xattn_bout", "L0_ffn_slot_query", "L0_ffn_d_Wq", "L0_ffn_d_Wk",
    "L0_ffn_d_Wv", "L0_ffn_d_Wo", "L0_ffn_d_bq", "L0_ffn_d_bk", "L0_ffn_d_bv", "L0_ffn_d_bo",
    "L0_ffn_c_Wq", "L0_ffn_c_Wk", "L0_ffn_c_Wv", "L0_ffn_c_Wo", "L0_ffn_c_bq", "L0_ffn_c_bk",
    "L0_ffn_c_bv", "L0_ffn_c_bo", "L0_ffn_e_ln_g", "L0_ffn_e_ln_b", "L0_ffn_e_W1", "L0_ffn_e_b1",
    "L0_ffn_e_Wg", "L0_ffn_e_bg", "L0_ffn_e_W2", "L0_ffn_e_b2", "L1_xattn_wq", "L1_xattn_wk",
    "L1_xattn_wv", "L1_xattn_fc_w", "L1_xattn_fc_b", "L1_xattn_rel_table", "L1_ffn_U1",
    "L1_ffn_V1", "L1_ffn_b1", "L1_ffn_U2", "L1_ffn_V2", "L1_ffn_b2", "L2_xattn_wq", "L2_xattn_wk",
    "L2_xattn_wv", "L2_xattn_bu", "L2_xattn_bv", "L2_xattn_wo", "L2_xattn_pos_w", "L2_ffn_weight",
    "L2_ffn_bias", "L3_xattn_w_sim", "L3_xattn_b_sim", "L3_xattn_W_qv", "L3_xattn_b_qv",
    "L3_ffn_gate_w", "L3_ffn_w1", "L3_ffn_b1", "L3_ffn_w2", "L3_ffn_b2", "L3_ffn_sw1",
    "L3_ffn_sb1", "L3_ffn_sw2", "L3_ffn_sb2",
)
_OUTS = [((128, 64, 128), 'float32')]


def kernel(**inputs):
    import numpy as _np
    import concourse.bacc as _bacc
    from concourse import mybir as _mybir
    from concourse.bass_utils import run_bass_kernel_spmd as _run

    nc = _bacc.Bacc("TRN2", target_bir_lowering=False, num_devices=1)
    arrays, names, args = {}, [], []
    for name in inputs:
        if name not in _USED:
            continue
        a = _np.ascontiguousarray(inputs[name])
        arrays[f"in_{name}_dram"] = a
        names.append(name)
        args.append(nc.dram_tensor(f"in_{name}_dram", a.shape, _mybir.dt.from_np(a.dtype), kind="ExternalInput").ap())
    for i, (shape, dtype) in enumerate(_OUTS):
        dt = _mybir.dt.from_np(_np.dtype(dtype))
        names.append("out")
        args.append(nc.dram_tensor(f"out_{i}_dram", shape, dt, kind="ExternalOutput").ap())
    build(nc, names, args)
    r = _run(nc, [arrays], core_ids=[0])
    return r.results[0]["out_0_dram"]
```
